# Optimizing a Trainium2 kernel written in Bass

```python
import numpy as np
import jax
import jax.numpy as jnp

def _softmax(x, axis=-1):
    return jax.nn.softmax(x, axis=axis)

def _gelu(x):
    return jax.nn.gelu(x, approximate=True)

def _silu(x):
    return jax.nn.silu(x)

def _sigmoid(x):
    return jax.nn.sigmoid(x)

def _layernorm(x, axis=-1, eps=1e-05):
    m = jnp.mean(x, axis=axis, keepdims=True)
    v = jnp.var(x, axis=axis, keepdims=True)
    return (x - m) / jnp.sqrt(v + eps)

def _scatter_add(tgt, idx, src, axis=0):
    return tgt.at[idx].add(src)

def _segment_sum(src, seg, n):
    return jax.ops.segment_sum(src, seg, n)
kernel_name = 'mk_adj_preln_d2_adj_r2_8f6950'

def setup_inputs(seed: int=0):
    np.random.seed(seed)
    _w = jnp.asarray

    def _rec_inputs():
        import jax
        import jax.numpy as jnp
        _gk = jax.random.key(seed)
        x = -0.0005207 + 1.001 * jax.random.normal(jax.random.fold_in(_gk, 1), (2048, 128), jnp.float32)
        _a = jax.random.bernoulli(jax.random.fold_in(_gk, 2), 0.0078125, (2048, 2048))
        _af = _a.astype(jnp.float32)
        adj = _af
        return (x, adj)
    x, adj = _rec_inputs()

    def _L0_gnn_setup():
        import jax, jax.numpy as jnp
        import numpy as np
        N = 8192
        U = 128
        AVG_DEGREE = 32
        key = jax.random.key(seed)
        kx, ka, kw = jax.random.split(key, 3)
        x = jax.random.normal(kx, (N, U), dtype=jnp.float32)
        adj = (jax.random.uniform(ka, (N, N)) < AVG_DEGREE / N).astype(jnp.float32)
        W = jax.random.normal(kw, (U, U), dtype=jnp.float32) * 0.05
        b = jnp.zeros((U,), dtype=jnp.float32)
        return {'x': x, 'adj': adj, 'W': W, 'b': b}
    _L0_gnn_all = _L0_gnn_setup()
    _L0_gnn_in = {k: v for k, v in _L0_gnn_all.items() if k in ('W', 'b')}
    del _L0_gnn_all

    def _L1_gnn_setup():
        import jax, jax.numpy as jnp
        import numpy as np
        N_NODE = 2048
        N_FEA_IN = 128
        N_FEA_OUT = 128
        key = jax.random.key(seed)
        k_x, k_a, k_w, k_att = jax.random.split(key, 4)
        stdv_w = 1.0 / np.sqrt(N_FEA_OUT)
        stdv_a = 1.0 / np.sqrt(2 * N_FEA_OUT)
        X = jax.random.normal(k_x, (N_NODE, N_FEA_IN), dtype=jnp.float32)
        A = jax.random.uniform(k_a, (N_NODE, N_NODE), dtype=jnp.float32)
        W = jax.random.uniform(k_w, (N_FEA_IN, N_FEA_OUT), minval=-stdv_w, maxval=stdv_w, dtype=jnp.float32)
        a = jax.random.uniform(k_att, (1, 2 * N_FEA_OUT), minval=-stdv_a, maxval=stdv_a, dtype=jnp.float32)
        return {'X': X, 'A': A, 'W': W, 'a': a}
    _L1_gnn_all = _L1_gnn_setup()
    _L1_gnn_in = {k: v for k, v in _L1_gnn_all.items() if k in ('W', 'a')}
    del _L1_gnn_all
    return {'x': x, 'adj': adj, 'L0_gnn_W': _L0_gnn_in['W'], 'L0_gnn_b': _L0_gnn_in['b'], 'L1_gnn_W': _L1_gnn_in['W'], 'L1_gnn_a': _L1_gnn_in['a']}

def reference(x, adj, L0_gnn_W, L0_gnn_b, L1_gnn_W, L1_gnn_a):
    import jax
    import jax.numpy as jnp

    def _L0_gnn_ref(x, adj, W, b):
        import jax, jax.numpy as jnp
        import numpy as np
        N = 8192
        U = 128
        AVG_DEGREE = 32
        adj = jax.lax.stop_gradient(adj)
        neigh1 = adj @ x
        x1 = jax.nn.swish(neigh1 @ W + b)
        neigh2 = adj @ x1
        x2 = jax.nn.swish(neigh2 @ W + b)
        return x2

    def _L1_gnn_ref(X, A, W, a):
        import jax, jax.numpy as jnp
        import numpy as np
        N_NODE = 2048
        N_FEA_IN = 128
        N_FEA_OUT = 128
        XW = jnp.matmul(X, W)
        f = W.shape[1]
        s_col = jnp.matmul(XW, a[0, :f])
        s_row = jnp.matmul(XW, a[0, f:])
        Z1 = jax.nn.leaky_relu(s_row[:, None] + s_col[None, :], negative_slope=0.01)
        den = jnp.exp(Z1)
        num = jnp.matmul(A, den)
        att = jnp.where(num != 0, den / jnp.where(num != 0, num, 1.0), 0.0)
        H = jnp.matmul(A, jnp.matmul(att, XW))
        return H
    h = jnp.maximum(_layernorm(x, axis=-1), 0.0)
    x = x + _L0_gnn_ref(h, adj, L0_gnn_W, L0_gnn_b)
    h = jnp.maximum(_layernorm(x, axis=-1), 0.0)
    x = x + _L1_gnn_ref(h, adj, L1_gnn_W, L1_gnn_a)
    return x

_drawn_inputs = setup_inputs


def setup_inputs(seed=0):
    import zlib

    import numpy as np

    out = dict(_drawn_inputs(seed))
    spreads = {'L0_gnn_b': (0.0, 0.1)}
    factors = {'L1_gnn_a': 6.568}
    for name, (base, spread) in spreads.items():
        noise = np.random.default_rng([zlib.crc32(name.encode()), seed]).standard_normal(out[name].shape)
        drawn = base * np.exp(spread * noise) if base else spread * noise
        out[name] = jnp.asarray(drawn.astype(out[name].dtype))
    for name, factor in factors.items():
        out[name] = (out[name] * factor).astype(out[name].dtype)
    return out
```

```python
import numpy as np
import concourse.bass as bass
import concourse.mybir as mybir

FP32 = mybir.dt.float32
ALU = mybir.AluOpType
ACT = mybir.ActivationFunctionType
AX = mybir.AxisListType

EPS = 1e-5
SLOPE = 0.01
P = 128
CH = 512


class Chain:

    def __init__(self, eng, sem):
        self.eng, self.sem, self.n = eng, sem, 0

    def step(self, instruction):
        self.n = self.n + 1
        instruction.then_inc(self.sem, 1)
        self.eng.wait_ge(self.sem, self.n)


def build(nc, x, adjT, W0, b0, W1, a1, outT):
    N, F = x.shape
    T = N // P
    C = N // CH
    sb = lambda name, shape: nc.alloc_sbuf_tensor(name, shape, FP32).ap()
    sem = lambda name: nc.alloc_semaphore(name)

    at_sb = sb("at_sb", [P, T, N])
    x_sb = sb("x_sb", [P, T, F])
    h_sb = sb("h_sb", [P, T, F])
    t_sb = sb("t_sb", [P, N])
    cb_sb = sb("cb_sb", [P, N])
    rb_sb = sb("rb_sb", [P, N])
    den_sb = [sb(f"den{i}_sb", [P, T, P]) for i in range(2)]
    dent_sb = sb("dent_sb", [P, N])
    num_sb = [sb(f"num{i}_sb", [P, CH]) for i in range(2)]
    zero_sb = sb("zero_sb", [P, P])
    rec_sb = sb("rec_sb", [P, CH])
    att_sb = [sb(f"att{i}_sb", [P, CH]) for i in range(2)]
    xwj_sb = [sb(f"xwj{i}_sb", [P, F]) for i in range(2)]
    w0_sb = sb("w0_sb", [F, F])
    w1_sb = sb("w1_sb", [F, F])
    b0_sb = sb("b0_sb", [1, F])
    ones_sb = sb("ones_sb", [1, P])
    a_sb = sb("a_sb", [F, 2])
    ab_sb = sb("ab_sb", [F, 2, P])
    rc_sb = sb("rc_sb", [P, T, 2])
    cj_sb = sb("cj_sb", [P, 1])
    ident = sb("ident", [P, P])
    stat = sb("stat", [P, 4, T])
    eps_sb = sb("eps_sb", [P, 1])

    psA = nc.alloc_psum_tensor("psA", [P, N], FP32).ap()
    psB = nc.alloc_psum_tensor("psB", [P, N], FP32).ap()

    s_ld = sem("s_loaded")
    s_adj = sem("s_adj_loaded")
    s_const = sem("s_const")
    s_ab = sem("s_a_broadcast")
    s_var = sem("s_variance")
    s_std = sem("s_std")
    s_h = sem("s_features_ready")
    s_prod = sem("s_product_done")
    s_t = sem("s_product_copied")
    s_wh = sem("s_dense_done")
    s_act = sem("s_swish_done")
    s_hT = sem("s_transposed")
    s_hTc = sem("s_transposed_copied")
    s_xwt = sem("s_xwt_done")
    s_xwtc = sem("s_xwt_copied")
    s_rc = sem("s_scores_done")
    s_rcc = sem("s_scores_copied")
    s_z = sem("s_z_ready")
    s_den = sem("s_den_ready")
    s_zt = sem("s_zt_ready")
    s_dent = sem("s_dent_ready")
    s_num = sem("s_num_done")
    s_numc = sem("s_num_copied")
    s_safe = sem("s_num_read")
    s_att = sem("s_att_ready")
    s_attused = sem("s_att_used")
    s_y = sem("s_y_done")
    s_yc = sem("s_y_copied")
    s_yn = sem("s_y_nodes")
    s_ync = sem("s_y_nodes_copied")
    s_out = sem("s_out")
    s_dve = sem("s_dve_chain")
    s_pool = sem("s_pool_chain")
    s_act_chain = sem("s_act_chain")

    x_d = x.rearrange("(t p) f -> p t f", p=P)
    at_d = adjT.rearrange("(t p) n -> p t n", p=P)

    with nc.Block() as block:

        @block.sync
        def _(sp):
            for dst, src in ((x_sb, x_d), (w0_sb, W0), (b0_sb, b0), (w1_sb, W1), (a_sb, a1)):
                sp.dma_start(dst, src).then_inc(s_ld, 16)
            for t in range(T):
                sp.dma_start(at_sb[:, t, :], at_d[:, t, :]).then_inc(s_adj, 16)
            for c in range(C):
                sp.wait_ge(s_t, 2 * C + c + 1)
                sp.dma_start(outT[:, c * CH:(c + 1) * CH], t_sb[:, c * CH:(c + 1) * CH]).then_inc(s_out, 16)
            sp.wait_ge(s_out, 16 * C)

        @block.gpsimd
        def _(pool):
            chain = Chain(pool, s_pool)
            pool.memset(eps_sb, EPS).then_inc(s_const, 1)
            pool.memset(ones_sb, 1.0).then_inc(s_const, 1)
            pool.memset(zero_sb, 0.0).then_inc(s_const, 1)
            chain.step(pool.memset(ident, 0.0))
            pool.affine_select(out=ident, in_=ident, compare_op=ALU.not_equal, fill=1.0, base=0,
                               pattern=[[-1, P]], channel_multiplier=1).then_inc(s_const, 1)

        @block.vector
        def _(dve):
            chain = Chain(dve, s_dve)

            def layernorm_relu(turn):
                mean, var, std, rstd = (stat[:, i, :] for i in range(4))
                chain.step(dve.tensor_reduce(mean, x_sb, axis=AX.X, op=ALU.add))
                chain.step(dve.tensor_scalar(mean, mean, 1.0 / F, None, ALU.mult))
                chain.step(dve.tensor_tensor(x_c, x_sb, mean.unsqueeze(2).to_broadcast([P, T, F]), ALU.subtract))
                chain.step(dve.tensor_tensor(h_sb, x_c, x_c, ALU.mult))
                chain.step(dve.tensor_reduce(var, h_sb, axis=AX.X, op=ALU.add))
                dve.tensor_scalar(var, var, 1.0 / F, EPS, ALU.mult, ALU.add).then_inc(s_var, 1)
                dve.wait_ge(s_std, turn + 1)
                chain.step(dve.reciprocal(rstd, std))
                dve.scalar_tensor_tensor(h_sb, x_c, 0.0, rstd.unsqueeze(2).to_broadcast([P, T, F]),
                                         ALU.max, ALU.mult).then_inc(s_h, 1)

            x_c = dent_sb.rearrange("p (t f) -> p t f", f=F)
            dve.wait_ge(s_ld, 5 * 16)
            dve.tensor_copy(ab_sb, a_sb.unsqueeze(2).to_broadcast([F, 2, P])).then_inc(s_ab, 1)
            layernorm_relu(0)
            for layer in range(2):
                for c in range(C):
                    dve.wait_ge(s_prod, layer * C + c + 1)
                    dve.tensor_copy(t_sb[:, c * CH:(c + 1) * CH], psA[:, c * CH:(c + 1) * CH]).then_inc(s_t, 1)
            dve.wait_ge(s_act, 2)
            chain.step(dve.tensor_tensor(x_sb, x_sb, h_sb, ALU.add))
            layernorm_relu(1)
            for c in range(C):
                dve.wait_ge(s_hT, c + 1)
                dve.tensor_copy(t_sb[:, c * CH:(c + 1) * CH], psA[:, c * CH:(c + 1) * CH]).then_inc(s_hTc, 1)
            dve.wait_ge(s_rc, 1)
            for c in range(C):
                dve.wait_ge(s_xwt, c + 1)
                dve.tensor_copy(t_sb[:, c * CH:(c + 1) * CH], psB[:, c * CH:(c + 1) * CH]).then_inc(s_xwtc, 1)
            dve.wait_ge(s_rc, 1)
            dve.tensor_copy(h_sb, psA.rearrange("p (t f) -> p t f", f=F)).then_inc(s_rcc, 1)
            dve.wait_ge(s_rc, 2)
            dve.tensor_copy(rc_sb, psB[:, 0:2 * T].rearrange("p (t o) -> p t o", o=2)).then_inc(s_rcc, 1)
            dve.wait_ge(s_rc, 3)
            dve.tensor_copy(cb_sb, psA).then_inc(s_rcc, 1)
            dve.wait_ge(s_rc, 4)
            chain.step(dve.tensor_copy(rb_sb, psB))
            dve.sem_inc(s_rcc, 1)

            base = chain.n
            steps = 5 + 3 * C
            with dve.Fori(0, T // 2) as i:
                for half in range(2):
                    jb = 2 * i + half
                    chain.n = base + jb * steps
                    cols = cb_sb[:, bass.ds(jb * P, P)].unsqueeze(1).to_broadcast([P, T, P])
                    rows = rc_sb[:, :, 1:2].to_broadcast([P, T, P])
                    chain.step(dve.tensor_tensor(den_sb[half], cols, rows, ALU.add))
                    dve.scalar_tensor_tensor(den_sb[half], den_sb[half], SLOPE, den_sb[half],
                                             ALU.mult, ALU.max).then_inc(s_z, 1)
                    chain.step(dve.tensor_copy(cj_sb, rc_sb[:, bass.ds(jb, 1), 0]))
                    chain.step(dve.tensor_copy(xwj_sb[half], h_sb[:, bass.ds(jb, 1), :].squeeze(1)))
                    chain.step(dve.tensor_scalar(dent_sb, rb_sb, cj_sb, None, ALU.add))
                    chain.step(dve.scalar_tensor_tensor(dent_sb, dent_sb, SLOPE, dent_sb, ALU.mult, ALU.max))
                    dve.sem_inc(s_zt, 1)
                    dve.wait_ge(s_dent, jb + 1)
                    for c in range(C):
                        q = jb * C + c
                        num = num_sb[c % 2]
                        dve.wait_ge(s_numc, q + C + 1)
                        dve.wait_ge(s_att, q + 2)
                        chain.step(dve.scalar_tensor_tensor(rec_sb, num, 0.0, num, ALU.is_equal, ALU.add))
                        chain.step(dve.reciprocal(rec_sb, rec_sb))
                        chain.step(dve.tensor_tensor(rec_sb, rec_sb, dent_sb[:, c * CH:(c + 1) * CH], ALU.mult))
                        dve.wait_ge(s_attused, q + 1)
                        dve.scalar_tensor_tensor(att_sb[c % 2], num, 0.0, rec_sb,
                                                 ALU.not_equal, ALU.mult).then_inc(s_att, 1)
            chain.n = base + T * steps
            for c in range(C):
                dve.wait_ge(s_y, c + 1)
                dve.tensor_copy(t_sb[:, c * CH:(c + 1) * CH], psB[:, c * CH:(c + 1) * CH]).then_inc(s_yc, 1)
            for c in range(C):
                dve.wait_ge(s_yn, c + 1)
                dve.tensor_copy(h_sb.rearrange("p t f -> p (t f)")[:, c * CH:(c + 1) * CH],
                                psA[:, c * CH:(c + 1) * CH]).then_inc(s_ync, 1)
            for c in range(C):
                dve.wait_ge(s_prod, 2 * C + c + 1)
                dve.tensor_copy(t_sb[:, c * CH:(c + 1) * CH], psB[:, c * CH:(c + 1) * CH]).then_inc(s_t, 1)

        @block.scalar
        def _(act):
            act.sem_inc(s_numc, C)
            act.wait_ge(s_const, 4)
            act.wait_ge(s_var, 1)
            act.activation(stat[:, 2, :], stat[:, 1, :], ACT.Sqrt).then_inc(s_std, 1)
            for layer in range(2):
                act.wait_ge(s_wh, layer + 1)
                act.activation(h_sb.rearrange("p t f -> p (t f)"), psB, ACT.Silu).then_inc(s_act, 1)
            act.wait_ge(s_var, 2)
            act.activation(stat[:, 2, :], stat[:, 1, :], ACT.Sqrt).then_inc(s_std, 1)
            with act.Fori(0, T // 2) as i:
                for half in range(2):
                    jb = 2 * i + half
                    act.wait_ge(s_z, jb + 1)
                    act.activation(den_sb[half], den_sb[half], ACT.Exp).then_inc(s_den, 1)
                    act.wait_ge(s_zt, jb + 1)
                    act.activation(dent_sb, dent_sb, ACT.Exp).then_inc(s_dent, 1)
                    for c in range(C):
                        q = jb * C + c
                        act.wait_ge(s_num, q + 1)
                        act.wait_ge(s_att, q + 1)
                        act.activation(num_sb[c % 2], psA[:, c * CH:(c + 1) * CH], ACT.Copy).then_inc(s_numc, 1)

        @block.tensor
        def _(pe):
            def propagate(ps, opened):
                with pe.Fori(0, C) as c:
                    for k in range(T):
                        mm = pe.matmul(ps[:, bass.ds(c * CH, CH)], h_sb[:, k, :], at_sb[:, k, bass.ds(c * CH, CH)],
                                       start=(k == 0 and not opened), stop=(k == T - 1))
                    mm.then_inc(s_prod, 1)

            pe.sem_inc(s_attused, 2)
            pe.sem_inc(s_att, 2)
            pe.wait_ge(s_const, 4)
            pe.wait_ge(s_adj, 16 * T)
            pe.wait_ge(s_h, 1)
            for layer in range(2):
                if layer == 1:
                    pe.wait_ge(s_act, 1)
                propagate(psA, False)
                pe.wait_ge(s_t, (layer + 1) * C)
                for t in range(T):
                    pe.matmul(psB[:, t * F:(t + 1) * F], t_sb[:, t * P:(t + 1) * P], w0_sb, start=True, stop=False)
                    mm = pe.matmul(psB[:, t * F:(t + 1) * F], ones_sb, b0_sb, start=False, stop=True)
                mm.then_inc(s_wh, 1)
            pe.wait_ge(s_h, 2)
            for t in range(T):
                tr = pe.transpose(psA[:, t * P:(t + 1) * P], h_sb[:, t, :], ident)
                if t % 4 == 3:
                    tr.then_inc(s_hT, 1)
            pe.wait_ge(s_hTc, C)
            for c in range(C):
                pe.matmul(psB[:, c * CH:(c + 1) * CH], w1_sb, t_sb[:, c * CH:(c + 1) * CH],
                          start=True, stop=True).then_inc(s_xwt, 1)
            for t in range(T):
                mm = pe.matmul(psA[:, t * F:(t + 1) * F], t_sb[:, t * P:(t + 1) * P], w1_sb, start=True, stop=True)
            mm.then_inc(s_rc, 1)
            pe.wait_ge(s_xwtc, C)
            pe.wait_ge(s_ab, 1)
            for t in range(T):
                mm = pe.matmul(psB[:, 2 * t:2 * t + 2], t_sb[:, t * P:(t + 1) * P], a_sb, start=True, stop=True)
            mm.then_inc(s_rc, 1)
            pe.wait_ge(s_rcc, 2)
            for side, ps in ((0, psA), (1, psB)):
                for c in range(C):
                    mm = pe.matmul(ps[:, c * CH:(c + 1) * CH], ab_sb[:, side, :], t_sb[:, c * CH:(c + 1) * CH],
                                   start=True, stop=True)
                mm.then_inc(s_rc, 1)
            pe.wait_ge(s_rcc, 4)
            for c in range(C):
                pe.matmul(psB[:, c * CH:(c + 1) * CH], zero_sb, at_sb[:, 0, c * CH:(c + 1) * CH],
                          start=True, stop=False)
            with pe.Fori(0, T // 2) as i:
                for half in range(2):
                    jb = 2 * i + half
                    pe.wait_ge(s_den, jb + 1)
                    for c in range(C):
                        q = jb * C + c
                        pe.wait_ge(s_numc, q + 1)
                        for k in range(T):
                            mm = pe.matmul(psA[:, c * CH:(c + 1) * CH], den_sb[half][:, k, :],
                                           at_sb[:, k, c * CH:(c + 1) * CH], start=(k == 0), stop=(k == T - 1))
                        mm.then_inc(s_num, 1)
                        if c > 0:
                            pe.wait_ge(s_att, q - 1 + 3)
                            pe.matmul(psB[:, (c - 1) * CH:c * CH], xwj_sb[half], att_sb[(c - 1) % 2],
                                      start=False, stop=False).then_inc(s_attused, 1)
                    pe.wait_ge(s_att, q + 3)
                    pe.matmul(psB[:, c * CH:(c + 1) * CH], xwj_sb[half], att_sb[c % 2],
                              start=False, stop=False).then_inc(s_attused, 1)
            for c in range(C):
                pe.matmul(psB[:, c * CH:(c + 1) * CH], zero_sb, at_sb[:, 0, c * CH:(c + 1) * CH],
                          start=False, stop=True).then_inc(s_y, 1)
            pe.wait_ge(s_yc, C)
            for t in range(T):
                tr = pe.transpose(psA[:, t * P:(t + 1) * P], t_sb[:, t * P:(t + 1) * P], ident)
                if t % 4 == 3:
                    tr.then_inc(s_yn, 1)
            for c in range(C):
                for t in range(4 * c, 4 * c + 4):
                    pe.matmul(psB[:, t * P:(t + 1) * P], x_sb[:, t, :], ident, start=(t % 4 == 0), stop=False)
            pe.wait_ge(s_ync, C)
            propagate(psB, True)


def kernel(x, adj, L0_gnn_W, L0_gnn_b, L1_gnn_W, L1_gnn_a):
    import concourse.bacc as bacc
    from concourse.bass_utils import run_bass_kernel_spmd

    x, adj, W0, b0, W1, a1 = (np.asarray(v) for v in (x, adj, L0_gnn_W, L0_gnn_b, L1_gnn_W, L1_gnn_a))
    F = x.shape[1]
    arrays = {
        "x": x, "adjT": np.ascontiguousarray(adj.T), "W0": W0, "b0": b0.reshape(1, F), "W1": W1,
        "a1": np.ascontiguousarray(a1.reshape(2, F).T),
    }
    nc = bacc.Bacc("TRN2", target_bir_lowering=False, num_devices=1)
    args = [nc.dram_tensor(n, v.shape, mybir.dt.from_np(v.dtype), kind="ExternalInput").ap()
            for n, v in arrays.items()]
    out = nc.dram_tensor("outT", (F, x.shape[0]), FP32, kind="ExternalOutput").ap()
    build(nc, *args, out)
    r = run_bass_kernel_spmd(nc, [arrays], core_ids=[0])
    return np.ascontiguousarray(r.results[0]["outT"].T)
```

```python
import numpy as np
import concourse.bass as bass
import concourse.mybir as mybir

FP32 = mybir.dt.float32
FP32R = mybir.dt.float32r
INT32 = mybir.dt.int32
ALU = mybir.AluOpType
ACT = mybir.ActivationFunctionType
AX = mybir.AxisListType

EPS = 1e-5
SLOPE = 0.01
P = 128
CH = 512
SCORE_LIMIT = 18.0


class Chain:

    def __init__(self, eng, sem):
        self.eng, self.sem, self.n = eng, sem, 0

    def step(self, instruction):
        self.n = self.n + 1
        instruction.then_inc(self.sem, 1)
        self.eng.wait_ge(self.sem, self.n)


class Buffers:
    pass


def buffers(nc, N, F):
    b = Buffers()
    b.N, b.F, b.T, b.C = N, F, N // P, N // CH
    T = b.T
    sb = lambda name, shape, dtype=FP32: nc.alloc_sbuf_tensor(name, shape, dtype).ap()
    b.w0_sb = sb("w0_sb", [F, F])
    b.w1_sb = sb("w1_sb", [F, F])
    b.b0_sb = sb("b0_sb", [1, F])
    b.ones_sb = sb("ones_sb", [P, P])
    b.zero_sb = sb("zero_sb", [P, P])
    b.ident = sb("ident", [P, P])
    b.a_sb = sb("a_sb", [F, 2])
    b.ab_sb = sb("ab_sb", [F, 2, P])
    b.rc_sb = sb("rc_sb", [P, T, 2])
    b.cj_sb = sb("cj_sb", [P, 1])
    b.cj2_sb = sb("cj2_sb", [P, 1])
    b.xwj_sb = [sb(f"xwj{i}_sb", [P, F]) for i in range(2)]
    b.stat = sb("stat", [P, 4, T])
    b.odd_sb = sb("odd_sb", [P, T + 1])
    b.sq_sb = sb("sq_sb", [P, T, 2])
    b.guard = sb("guard", [P, 4])
    b.tiny_sb = sb("tiny_sb", [P, 1])
    b.need_general = sb("need_general", [P, 1], INT32)[0:1, :]
    b.go_fast = sb("go_fast", [P, 1], INT32)[0:1, :]
    b.at_off = -(-nc.sbuf_base // 32) * 32
    slot_bytes = 4 * N
    nc.alloc_sbuf_tensor("arena", [P, (T + 9) * N], FP32)
    b.at = lambda name, shape, offset, dtype=FP32: nc.alloc_sbuf_tensor_at(name, shape, dtype, offset=offset).ap()
    b.slot = lambda name, shape, n, part=0, dtype=FP32: b.at(
        name, shape, b.at_off + (T + n) * slot_bytes + part * 4 * CH, dtype)
    b.x_sb = b.slot("x_sb", [P, T, F], 0)
    b.psA = nc.alloc_psum_tensor("psA", [P, N], FP32).ap()
    b.psB = nc.alloc_psum_tensor("psB", [P, N], FP32).ap()
    return b


def build_fast(nc, b, x, adjT, W0, b0, W1, a1, outT):
    N, F, T, C = b.N, b.F, b.T, b.C
    sem = lambda name: nc.alloc_semaphore(name)
    psA, psB, ident, stat, x_sb = b.psA, b.psB, b.ident, b.stat, b.x_sb
    flat = lambda ap: ap.rearrange("p t f -> p (t f)")
    chunk = lambda ap, c: ap[:, c * CH:(c + 1) * CH]

    at_r = b.at("at_r", [P, T, N], b.at_off, FP32R)
    raw = [b.slot(f"raw{i}", [P, N], 4 + i) for i in range(3)]
    odd = [b.slot(f"odd{i}", [P, N], 7 + i) for i in range(2)]
    hi_r = b.slot("hi_r", [P, T, F], 1, dtype=FP32R)
    lo_r = b.slot("lo_r", [P, T, F], 2, dtype=FP32R)
    t_sb = b.slot("t_sb", [P, N], 3)
    xc0_sb = b.slot("xc0_sb", [P, T, F], 3)
    h0_sb = b.slot("h0_sb", [P, T, F], 8)
    h_sb = b.slot("h_sb", [P, T, F], 4)
    xc_sb = b.slot("xc_sb", [P, T, F], 5)
    ht_sb = b.slot("ht_sb", [P, N], 6)
    xwt_sb = b.slot("xwt_sb", [P, N], 7)
    xw_sb = b.slot("xw_sb", [P, T, F], 1)
    rb_sb = b.slot("rb_sb", [P, N], 2)
    cb_sb = b.slot("cb_sb", [P, N], 3)
    zt_sb = [b.slot(f"zt{i}_sb", [P, CH], 4, part=i) for i in range(2)]
    att_sb = [b.slot(f"att{i}_sb", [P, CH], 4, part=2 + i) for i in range(2)]
    den_hi = [b.slot(f"den_hi{i}", [P, T, P], 5 + 2 * i, dtype=FP32R) for i in range(2)]
    den_lo = [b.slot(f"den_lo{i}", [P, T, P], 6 + 2 * i, dtype=FP32R) for i in range(2)]
    den_sb = [b.slot(f"den{i}_sb", [P, T, P], 6 + 2 * i) for i in range(2)]
    sq_sb = b.sq_sb
    cj_sb = (b.cj_sb, b.cj2_sb)
    mask_sb = b.slot("mask_sb", [P, N], 3)
    yt_sb = b.slot("yt_sb", [P, N], 2)
    y_hi = b.slot("y_hi", [P, T, F], 5, dtype=FP32R)
    y_lo = b.slot("y_lo", [P, T, F], 6, dtype=FP32R)
    out_sb = b.slot("out_sb", [P, N], 3)

    s_ld = sem("s_loaded")
    s_raw = [sem(f"s_raw{i}_loaded") for i in range(3)]
    s_const = sem("s_const")
    s_ab = sem("s_a_broadcast")
    s_var = sem("s_variance")
    s_std = sem("s_std")
    s_split = sem("s_features_split")
    s_odd = sem("s_odd_terms")
    s_oddsum = sem("s_odd_terms_summed")
    s_ard = sem("s_tile_by_dve")
    s_ara = sem("s_tile_by_act")
    s_prod = sem("s_product_done")
    s_t = sem("s_product_copied")
    s_wh = sem("s_dense_done")
    s_act = sem("s_swish_done")
    s_h = sem("s_normalised")
    s_hT = sem("s_transposed")
    s_hTc = sem("s_transposed_copied")
    s_xwt = sem("s_xwt_done")
    s_xwtc = sem("s_xwt_copied")
    s_rc = sem("s_scores_done")
    s_rcc = sem("s_scores_copied")
    s_rng = sem("s_range_terms")
    s_oddall = sem("s_odd_total")
    s_z = sem("s_z_ready")
    s_den = sem("s_den_ready")
    s_denhi = sem("s_den_high_ready")
    s_denlo = sem("s_den_low_ready")
    s_xwj = sem("s_xw_block_ready")
    s_zt = sem("s_zt_ready")
    s_num = sem("s_num_done")
    s_ln = sem("s_ln_ready")
    s_sub = sem("s_logit_ready")
    s_att = sem("s_att_ready")
    s_attused = sem("s_att_used")
    s_mask = sem("s_mask_ready")
    s_y = sem("s_y_done")
    s_yc = sem("s_y_copied")
    s_yn = sem("s_y_nodes")
    s_ync = sem("s_y_nodes_split")
    s_out = sem("s_out")
    s_dve = sem("s_dve_chain")
    s_dve2 = sem("s_dve_chain2")
    s_pool = sem("s_pool_chain")

    x_d = x.rearrange("(t p) f -> p t f", p=P)
    by_act = [t % 2 == 1 for t in range(T)]

    with nc.Block() as block:

        @block.sync
        def _(sp):
            for dst, src in ((x_sb, x_d), (b.w0_sb, W0), (b.b0_sb, b0), (b.w1_sb, W1), (b.a_sb, a1)):
                sp.dma_start(dst, src).then_inc(s_ld, 16)
            for t in range(T):
                if t >= 3:
                    sp.wait_ge(s_odd, t - 2)
                    sp.wait_ge(s_ara if by_act[t - 3] else s_ard, (t - 3) // 2 + 1)
                sp.dma_start(raw[t % 3], adjT[t * P:(t + 1) * P, :]).then_inc(s_raw[t % 3], 16)

        @block.gpsimd
        def _(pool):
            chain = Chain(pool, s_pool)
            pool.memset(b.ones_sb, 1.0).then_inc(s_const, 1)
            pool.memset(b.zero_sb, 0.0).then_inc(s_const, 1)
            pool.memset(b.tiny_sb, 1e-15).then_inc(s_const, 1)
            chain.step(pool.memset(ident, 0.0))
            pool.affine_select(out=ident, in_=ident, compare_op=ALU.not_equal, fill=1.0, base=0,
                               pattern=[[-1, P]], channel_multiplier=1).then_inc(s_const, 1)

        @block.vector
        def _(dve):
            chain = Chain(dve, s_dve)

            def layernorm_relu(turn, h, x_c):
                mean, var, std, rstd = (stat[:, i, :] for i in range(4))
                chain.step(dve.tensor_reduce(mean, x_sb, axis=AX.X, op=ALU.add))
                chain.step(dve.tensor_scalar(mean, mean, 1.0 / F, None, ALU.mult))
                chain.step(dve.tensor_tensor(x_c, x_sb, mean.unsqueeze(2).to_broadcast([P, T, F]), ALU.subtract))
                chain.step(dve.tensor_tensor(h, x_c, x_c, ALU.mult))
                chain.step(dve.tensor_reduce(var, h, axis=AX.X, op=ALU.add))
                dve.tensor_scalar(var, var, 1.0 / F, EPS, ALU.mult, ALU.add).then_inc(s_var, 1)
                dve.wait_ge(s_std, turn + 1)
                chain.step(dve.reciprocal(rstd, std))
                dve.scalar_tensor_tensor(h, x_c, 0.0, rstd.unsqueeze(2).to_broadcast([P, T, F]),
                                         ALU.max, ALU.mult).then_inc(s_h, 1)
                dve.wait_ge(s_h, turn + 1)

            def split(src, part, hi, lo):
                chain.step(dve.tensor_copy(hi[:, part], src[:, part]))
                dve.tensor_tensor(lo[:, part], src[:, part], hi[:, part].bitcast(FP32),
                                  ALU.subtract).then_inc(s_split, 1)

            dve.wait_ge(s_ld, 5 * 16)
            dve.tensor_copy(b.ab_sb, b.a_sb.unsqueeze(2).to_broadcast([F, 2, P])).then_inc(s_ab, 1)
            layernorm_relu(0, h0_sb, xc0_sb)
            split(h0_sb, slice(0, T), hi_r, lo_r)
            dve.wait_ge(s_split, 1)
            for t in range(T):
                dve.wait_ge(s_raw[t % 3], 16 * (t // 3 + 1))
                if t >= 2:
                    dve.wait_ge(s_oddsum, t - 1)
                dve.scalar_tensor_tensor(odd[t % 2], raw[t % 3], 1.0, raw[t % 3],
                                         ALU.subtract, ALU.mult).then_inc(s_odd, 1)
                if not by_act[t]:
                    dve.tensor_copy(at_r[:, t, :], raw[t % 3]).then_inc(s_ard, 1)
            for layer in range(2):
                for c in range(C):
                    dve.wait_ge(s_prod, layer * C + c + 1)
                    dve.tensor_copy(chunk(t_sb, c), chunk(psA, c)).then_inc(s_t, 1)
                if layer == 0:
                    for c in range(C):
                        dve.wait_ge(s_act, c + 1)
                        split(h_sb, slice(c * T // C, (c + 1) * T // C), hi_r, lo_r)
            dve.wait_ge(s_act, 2 * C)
            chain.step(dve.tensor_tensor(x_sb, x_sb, h_sb, ALU.add))
            layernorm_relu(1, h_sb, xc_sb)
            for c in range(C):
                dve.wait_ge(s_hT, c + 1)
                dve.tensor_copy(chunk(ht_sb, c), chunk(psA, c)).then_inc(s_hTc, 1)
            for c in range(C):
                dve.wait_ge(s_xwt, c + 1)
                dve.tensor_copy(chunk(xwt_sb, c), chunk(psB, c)).then_inc(s_xwtc, 1)
            dve.wait_ge(s_rc, 1)
            dve.tensor_copy(flat(xw_sb), psA).then_inc(s_rcc, 1)
            dve.wait_ge(s_rc, 2)
            dve.tensor_copy(b.rc_sb, psB[:, 0:2 * T].rearrange("p (t o) -> p t o", o=2)).then_inc(s_rcc, 1)
            dve.wait_ge(s_rc, 3)
            dve.tensor_copy(cb_sb, psA).then_inc(s_rcc, 1)
            dve.wait_ge(s_rc, 4)
            dve.tensor_copy(rb_sb, psB).then_inc(s_rcc, 1)
            dve.wait_ge(s_rcc, 4)

            chain.step(dve.tensor_tensor(sq_sb, b.rc_sb, b.rc_sb, ALU.mult))
            chain.step(dve.tensor_scalar(sq_sb, sq_sb, SCORE_LIMIT ** 2, None, ALU.is_le))
            chain.step(dve.tensor_scalar(sq_sb, sq_sb, -1.0, 1.0, ALU.mult, ALU.add))
            dve.tensor_reduce(b.odd_sb[:, T:T + 1], sq_sb, axis=AX.XY, op=ALU.add).then_inc(s_rng, 1)
            g = b.guard
            dve.wait_ge(s_oddall, 1)
            chain.step(dve.tensor_reduce(g[:, 0:1], psA[:, 0:T + 1], axis=AX.X, op=ALU.add))
            chain.step(dve.tensor_scalar(g[:, 1:2], g[:, 0:1], 0.0, None, ALU.is_le))
            dve.tensor_copy(b.go_fast, g[0:1, 1:2])
            dve.tensor_scalar(b.need_general, g[0:1, 1:2], -1.0, 1.0, ALU.mult, ALU.add)

        @block.scalar
        def _(act):
            act.wait_ge(s_const, 4)
            act.wait_ge(s_var, 1)
            act.activation(stat[:, 2, :], stat[:, 1, :], ACT.Sqrt).then_inc(s_std, 1)
            for t in range(T):
                if by_act[t]:
                    act.wait_ge(s_raw[t % 3], 16 * (t // 3 + 1))
                    act.activation(at_r[:, t, :], raw[t % 3], ACT.Copy).then_inc(s_ara, 1)
                act.wait_ge(s_odd, t + 1)
                act.activation(odd[t % 2], odd[t % 2], ACT.Abs,
                               accum_out=b.odd_sb[:, t:t + 1]).then_inc(s_oddsum, 1)
            for layer in range(2):
                for c in range(C):
                    act.wait_ge(s_wh, layer * C + c + 1)
                    act.activation(chunk(flat(h_sb), c), chunk(psB, c), ACT.Silu).then_inc(s_act, 1)
            act.wait_ge(s_var, 2)
            act.activation(stat[:, 2, :], stat[:, 1, :], ACT.Sqrt).then_inc(s_std, 1)

        @block.tensor
        def _(pe):

            def dense(layer):
                for c in range(C):
                    pe.wait_ge(s_t, layer * C + c + 1)
                    for t in range(c * T // C, (c + 1) * T // C):
                        out = psB[:, t * F:(t + 1) * F]
                        pe.matmul(out, t_sb[:, t * P:(t + 1) * P], b.w0_sb, start=True, stop=False)
                        mm = pe.matmul(out, b.ones_sb[0:1, :], b.b0_sb, start=False, stop=True)
                    mm.then_inc(s_wh, 1)

            def product(ps, t, hi, lo, start, stop):
                for c in range(C):
                    pe.matmul(chunk(ps, c), hi[:, t, :], at_r[:, t, c * CH:(c + 1) * CH],
                              start=start, stop=False)
                    mm = pe.matmul(chunk(ps, c), lo[:, t, :], at_r[:, t, c * CH:(c + 1) * CH],
                                   start=False, stop=stop)
                    if stop:
                        mm.then_inc(s_prod, 1)

            pe.wait_ge(s_const, 4)
            pe.wait_ge(s_split, 1)
            for t in range(T):
                pe.wait_ge(s_ara if by_act[t] else s_ard, t // 2 + 1)
                product(psA, t, hi_r, lo_r, t == 0, t == T - 1)
            dense(0)
            for t in range(T):
                if t % (T // C) == 0:
                    pe.wait_ge(s_split, 1 + t // (T // C) + 1)
                product(psA, t, hi_r, lo_r, t == 0, t == T - 1)
            dense(1)
            pe.wait_ge(s_h, 2)
            for t in range(T):
                tr = pe.transpose(psA[:, t * P:(t + 1) * P], h_sb[:, t, :], ident)
                if t % 4 == 3:
                    tr.then_inc(s_hT, 1)
            for c in range(C):
                pe.wait_ge(s_hTc, c + 1)
                pe.matmul(chunk(psB, c), b.w1_sb, chunk(ht_sb, c), start=True, stop=True).then_inc(s_xwt, 1)
            for t in range(T):
                mm = pe.matmul(psA[:, t * F:(t + 1) * F], ht_sb[:, t * P:(t + 1) * P], b.w1_sb, start=True, stop=True)
            mm.then_inc(s_rc, 1)
            pe.wait_ge(s_xwtc, C)
            pe.wait_ge(s_ab, 1)
            for t in range(T):
                mm = pe.matmul(psB[:, 2 * t:2 * t + 2], xwt_sb[:, t * P:(t + 1) * P], b.a_sb, start=True, stop=True)
            mm.then_inc(s_rc, 1)
            for side, ps in ((0, psA), (1, psB)):
                pe.wait_ge(s_rcc, side + 1)
                for c in range(C):
                    mm = pe.matmul(chunk(ps, c), b.ab_sb[:, side, :], chunk(xwt_sb, c), start=True, stop=True)
                mm.then_inc(s_rc, 1)
            pe.wait_ge(s_rcc, 4)
            pe.wait_ge(s_rng, 1)
            pe.wait_ge(s_rcc, 3)
            pe.matmul(psA[:, 0:T + 1], b.ones_sb, b.odd_sb, start=True, stop=True).then_inc(s_oddall, 1)

    with nc.Block() as block:

        @block.sync
        def _(sp):
            with sp.If(sp.value_load(b.go_fast, min_val=0, max_val=1)):
                for c in range(C):
                    sp.wait_ge(s_t, 3 * C - C + c + 1)
                    sp.dma_start(chunk(outT, c), chunk(out_sb, c)).then_inc(s_out, 16)
                sp.wait_ge(s_out, 16 * C)

        @block.gpsimd
        def _(pool):
            with pool.If(pool.value_load(b.go_fast, min_val=0, max_val=1)):
                with pool.Fori(0, T // 2) as i:
                    for half in range(2):
                        jb = 2 * i + half
                        pool.wait_ge(s_attused, (jb + 1) * C)
                        pool.tensor_copy(b.xwj_sb[half], xw_sb[:, bass.ds(jb, 1), :].squeeze(1)).then_inc(s_xwj, 1)
                        pool.tensor_copy(cj_sb[half], b.rc_sb[:, bass.ds(jb, 1), 0]).then_inc(s_xwj, 1)

        @block.vector
        def _(dve):
            with dve.If(dve.value_load(b.go_fast, min_val=0, max_val=1)):
                chain = Chain(dve, s_dve2)
                base = chain.n

                def den_scores(jb, half):
                    chain.n = base + jb
                    cols = cb_sb[:, bass.ds(jb * P, P)].unsqueeze(1).to_broadcast([P, T, P])
                    rows = b.rc_sb[:, :, 1:2].to_broadcast([P, T, P])
                    chain.step(dve.tensor_tensor(den_sb[half], cols, rows, ALU.add))
                    dve.scalar_tensor_tensor(den_sb[half], den_sb[half], SLOPE, den_sb[half],
                                             ALU.mult, ALU.max).then_inc(s_z, 1)

                def den_low(jb, half):
                    dve.wait_ge(s_denhi, jb + 1)
                    dve.tensor_tensor(den_lo[half], den_sb[half], den_hi[half].bitcast(FP32),
                                      ALU.subtract).then_inc(s_denlo, 1)

                def block(jb, half, more):
                    if more:
                        dve.wait_ge(s_num, (jb + 2) * C)
                        den_scores(jb + 1, 1 - half)
                    dve.wait_ge(s_xwj, 2 * jb + 2)
                    for c in range(C):
                        q = jb * C + c
                        dve.wait_ge(s_sub, q - 1 + C)
                        dve.tensor_scalar(zt_sb[c % 2], chunk(rb_sb, c), cj_sb[half], None, ALU.add).then_inc(s_zt, 1)
                        dve.wait_ge(s_zt, 2 * q + 1)
                        dve.scalar_tensor_tensor(zt_sb[c % 2], zt_sb[c % 2], SLOPE, zt_sb[c % 2],
                                                 ALU.mult, ALU.max).then_inc(s_zt, 1)
                        if c == 1 and more:
                            den_low(jb + 1, 1 - half)
                        dve.wait_ge(s_attused, q - 1 + 2 * C)
                        dve.wait_ge(s_zt, 2 * q + 2)
                        dve.wait_ge(s_ln, q + 1)
                        dve.tensor_tensor(att_sb[c % 2], zt_sb[c % 2], chunk(psA, c),
                                          ALU.subtract).then_inc(s_sub, 1)

                den_scores(0, 0)
                den_low(0, 0)
                with dve.Fori(0, T // 2 - 1) as i:
                    for half in range(2):
                        block(2 * i + half, half, True)
                block(T - 2, 0, True)
                block(T - 1, 1, False)
                chain.n = base + T
                for c in range(C):
                    chain.step(dve.tensor_scalar(chunk(mask_sb, c), chunk(psA, c), -20.0, None, ALU.is_gt))
                    dve.wait_ge(s_y, c + 1)
                    dve.tensor_tensor(chunk(yt_sb, c), chunk(psB, c), chunk(mask_sb, c), ALU.mult).then_inc(s_yc, 1)
                for c in range(C):
                    dve.wait_ge(s_yn, c + 1)
                    part = slice(c * T // C, (c + 1) * T // C)
                    chain.step(dve.tensor_copy(flat(y_hi[:, part]), chunk(psA, c)))
                    dve.tensor_tensor(flat(y_lo[:, part]), chunk(psA, c), flat(y_hi[:, part].bitcast(FP32)),
                                      ALU.subtract).then_inc(s_ync, 1)
                for c in range(C):
                    dve.wait_ge(s_prod, 2 * C + c + 1)
                    dve.tensor_copy(chunk(out_sb, c), chunk(psB, c)).then_inc(s_t, 1)

        @block.scalar
        def _(act):
            with act.If(act.value_load(b.go_fast, min_val=0, max_val=1)):

                def den_exp(jb, half):
                    act.wait_ge(s_z, jb + 1)
                    act.activation(den_sb[half], den_sb[half], ACT.Exp).then_inc(s_den, 1)
                    act.wait_ge(s_den, jb + 1)
                    act.activation(den_hi[half], den_sb[half], ACT.Copy).then_inc(s_denhi, 1)

                def block(jb, half, more):
                    if more:
                        den_exp(jb + 1, 1 - half)
                    for c in range(C):
                        q = jb * C + c
                        act.wait_ge(s_num, q + 2 * C + 1)
                        act.activation(chunk(psA, c), chunk(psA, c), ACT.Ln, bias=b.tiny_sb).then_inc(s_ln, 1)
                        act.wait_ge(s_sub, q + 1 + C)
                        act.activation(att_sb[c % 2], att_sb[c % 2], ACT.Exp).then_inc(s_att, 1)

                den_exp(0, 0)
                with act.Fori(0, T // 2 - 1) as i:
                    for half in range(2):
                        block(2 * i + half, half, True)
                block(T - 2, 0, True)
                block(T - 1, 1, False)

        @block.tensor
        def _(pe):
            with pe.If(pe.value_load(b.go_fast, min_val=0, max_val=1)):
                pe.sem_inc(s_num, 2 * C)
                pe.sem_inc(s_attused, 2 * C)
                pe.sem_inc(s_sub, C)
                for c in range(C):
                    pe.matmul(chunk(psB, c), b.zero_sb, chunk(rb_sb, c), start=True, stop=False)
                with pe.Fori(0, T // 2) as i:
                    for half in range(2):
                        jb = 2 * i + half
                        pe.wait_ge(s_denlo, jb + 1)
                        pe.wait_ge(s_xwj, 2 * jb + 2)

                        def use(c, q):
                            pe.wait_ge(s_att, q + 1)
                            pe.matmul(chunk(psB, c), b.xwj_sb[half], att_sb[c % 2],
                                      start=False, stop=False).then_inc(s_attused, 1)

                        for c in range(C):
                            q = jb * C + c
                            pe.wait_ge(s_sub, q + 1)
                            for k in range(T):
                                rhs = at_r[:, k, c * CH:(c + 1) * CH]
                                pe.matmul(chunk(psA, c), den_hi[half][:, k, :], rhs, start=(k == 0), stop=False)
                                mm = pe.matmul(chunk(psA, c), den_lo[half][:, k, :], rhs, start=False, stop=(k == T - 1))
                            mm.then_inc(s_num, 1)
                            if c > 0:
                                use(c - 1, q - 1)
                        use(C - 1, q)
                for c in range(C):
                    pe.matmul(chunk(psB, c), b.zero_sb, chunk(rb_sb, c), start=False, stop=True).then_inc(s_y, 1)
                for c in range(C):
                    pe.wait_ge(s_yc, c + 1)
                    for t in range(4 * c, 4 * c + 4):
                        tr = pe.transpose(psA[:, t * P:(t + 1) * P], yt_sb[:, t * P:(t + 1) * P], ident)
                    tr.then_inc(s_yn, 1)
                for c in range(C):
                    for t in range(4 * c, 4 * c + 4):
                        pe.matmul(psB[:, t * P:(t + 1) * P], x_sb[:, t, :], ident, start=(t % 4 == 0), stop=False)
                pe.wait_ge(s_ync, C)
                for t in range(T):
                    for c in range(C):
                        pe.matmul(chunk(psB, c), y_hi[:, t, :], at_r[:, t, c * CH:(c + 1) * CH], start=False, stop=False)
                        mm = pe.matmul(chunk(psB, c), y_lo[:, t, :], at_r[:, t, c * CH:(c + 1) * CH],
                                       start=False, stop=(t == T - 1))
                        if t == T - 1:
                            mm.then_inc(s_prod, 1)


def build_general(nc, b, x, adjT, outT):
    N, F, T, C = b.N, b.F, b.T, b.C
    sem = lambda name: nc.alloc_semaphore("g_" + name)
    at_sb = b.at("g_at_sb", [P, T, N], b.at_off)
    x_sb = b.x_sb
    h_sb = b.slot("g_h_sb", [P, T, F], 1)
    t_sb = b.slot("g_t_sb", [P, N], 2)
    cb_sb = b.slot("g_cb_sb", [P, N], 3)
    rb_sb = b.slot("g_rb_sb", [P, N], 4)
    den_sb = [b.slot(f"g_den{i}_sb", [P, T, P], 5 + i) for i in range(2)]
    dent_sb = b.slot("g_dent_sb", [P, N], 7)
    num_sb = [b.slot(f"g_num{i}_sb", [P, CH], 8, part=i) for i in range(2)]
    rec_sb = b.slot("g_rec_sb", [P, CH], 8, part=2)
    att_sb = b.slot("g_att_sb", [P, CH], 8, part=3)
    w0_sb, w1_sb, b0_sb, ones_sb, zero_sb, a_sb, ab_sb, rc_sb, cj_sb, ident, stat, xwj_sb = (
        b.w0_sb, b.w1_sb, b.b0_sb, b.ones_sb, b.zero_sb, b.a_sb, b.ab_sb, b.rc_sb, b.cj_sb, b.ident, b.stat, b.xwj_sb)
    psA, psB = b.psA, b.psB
    s_ld = sem("s_loaded")
    s_adj = sem("s_adj_loaded")
    s_var = sem("s_variance")
    s_std = sem("s_std")
    s_h = sem("s_features_ready")
    s_prod = sem("s_product_done")
    s_t = sem("s_product_copied")
    s_wh = sem("s_dense_done")
    s_act = sem("s_swish_done")
    s_hT = sem("s_transposed")
    s_hTc = sem("s_transposed_copied")
    s_xwt = sem("s_xwt_done")
    s_xwtc = sem("s_xwt_copied")
    s_rc = sem("s_scores_done")
    s_rcc = sem("s_scores_copied")
    s_z = sem("s_z_ready")
    s_den = sem("s_den_ready")
    s_zt = sem("s_zt_ready")
    s_dent = sem("s_dent_ready")
    s_num = sem("s_num_done")
    s_numc = sem("s_num_copied")
    s_safe = sem("s_num_read")
    s_att = sem("s_att_ready")
    s_attused = sem("s_att_used")
    s_y = sem("s_y_done")
    s_yc = sem("s_y_copied")
    s_yn = sem("s_y_nodes")
    s_ync = sem("s_y_nodes_copied")
    s_out = sem("s_out")
    s_dve = sem("s_dve_chain")

    x_d = x.rearrange("(t p) f -> p t f", p=P)
    at_d = adjT.rearrange("(t p) n -> p t n", p=P)

    with nc.Block() as block:

        @block.sync
        def _(sp):
            with sp.If(sp.value_load(b.need_general, min_val=0, max_val=1)):
                sp.dma_start(x_sb, x_d).then_inc(s_ld, 16)
                for t in range(T):
                    sp.dma_start(at_sb[:, t, :], at_d[:, t, :]).then_inc(s_adj, 16)
                for c in range(C):
                    sp.wait_ge(s_t, 2 * C + c + 1)
                    sp.dma_start(outT[:, c * CH:(c + 1) * CH], t_sb[:, c * CH:(c + 1) * CH]).then_inc(s_out, 16)
                sp.wait_ge(s_out, 16 * C)

        @block.vector
        def _(dve):
            with dve.If(dve.value_load(b.need_general, min_val=0, max_val=1)):
                chain = Chain(dve, s_dve)

                def layernorm_relu(turn):
                    mean, var, std, rstd = (stat[:, i, :] for i in range(4))
                    chain.step(dve.tensor_reduce(mean, x_sb, axis=AX.X, op=ALU.add))
                    chain.step(dve.tensor_scalar(mean, mean, 1.0 / F, None, ALU.mult))
                    chain.step(dve.tensor_tensor(x_c, x_sb, mean.unsqueeze(2).to_broadcast([P, T, F]), ALU.subtract))
                    chain.step(dve.tensor_tensor(h_sb, x_c, x_c, ALU.mult))
                    chain.step(dve.tensor_reduce(var, h_sb, axis=AX.X, op=ALU.add))
                    dve.tensor_scalar(var, var, 1.0 / F, EPS, ALU.mult, ALU.add).then_inc(s_var, 1)
                    dve.wait_ge(s_std, turn + 1)
                    chain.step(dve.reciprocal(rstd, std))
                    dve.scalar_tensor_tensor(h_sb, x_c, 0.0, rstd.unsqueeze(2).to_broadcast([P, T, F]),
                                             ALU.max, ALU.mult).then_inc(s_h, 1)

                x_c = dent_sb.rearrange("p (t f) -> p t f", f=F)
                dve.wait_ge(s_ld, 16)
                layernorm_relu(0)
                for layer in range(2):
                    for c in range(C):
                        dve.wait_ge(s_prod, layer * C + c + 1)
                        dve.tensor_copy(t_sb[:, c * CH:(c + 1) * CH], psA[:, c * CH:(c + 1) * CH]).then_inc(s_t, 1)
                dve.wait_ge(s_act, 2)
                chain.step(dve.tensor_tensor(x_sb, x_sb, h_sb, ALU.add))
                layernorm_relu(1)
                for c in range(C):
                    dve.wait_ge(s_hT, c + 1)
                    dve.tensor_copy(t_sb[:, c * CH:(c + 1) * CH], psA[:, c * CH:(c + 1) * CH]).then_inc(s_hTc, 1)
                dve.wait_ge(s_rc, 1)
                for c in range(C):
                    dve.wait_ge(s_xwt, c + 1)
                    dve.tensor_copy(t_sb[:, c * CH:(c + 1) * CH], psB[:, c * CH:(c + 1) * CH]).then_inc(s_xwtc, 1)
                dve.wait_ge(s_rc, 1)
                dve.tensor_copy(h_sb, psA.rearrange("p (t f) -> p t f", f=F)).then_inc(s_rcc, 1)
                dve.wait_ge(s_rc, 2)
                dve.tensor_copy(rc_sb, psB[:, 0:2 * T].rearrange("p (t o) -> p t o", o=2)).then_inc(s_rcc, 1)
                dve.wait_ge(s_rc, 3)
                dve.tensor_copy(cb_sb, psA).then_inc(s_rcc, 1)
                dve.wait_ge(s_rc, 4)
                chain.step(dve.tensor_copy(rb_sb, psB))
                dve.sem_inc(s_rcc, 1)

                base = chain.n
                steps = 5 + 3 * C
                with dve.Fori(0, T // 2) as i:
                    for half in range(2):
                        jb = 2 * i + half
                        chain.n = base + jb * steps
                        cols = cb_sb[:, bass.ds(jb * P, P)].unsqueeze(1).to_broadcast([P, T, P])
                        rows = rc_sb[:, :, 1:2].to_broadcast([P, T, P])
                        chain.step(dve.tensor_tensor(den_sb[half], cols, rows, ALU.add))
                        dve.scalar_tensor_tensor(den_sb[half], den_sb[half], SLOPE, den_sb[half],
                                                 ALU.mult, ALU.max).then_inc(s_z, 1)
                        chain.step(dve.tensor_copy(cj_sb, rc_sb[:, bass.ds(jb, 1), 0]))
                        chain.step(dve.tensor_copy(xwj_sb[half], h_sb[:, bass.ds(jb, 1), :].squeeze(1)))
                        chain.step(dve.tensor_scalar(dent_sb, rb_sb, cj_sb, None, ALU.add))
                        chain.step(dve.scalar_tensor_tensor(dent_sb, dent_sb, SLOPE, dent_sb, ALU.mult, ALU.max))
                        dve.sem_inc(s_zt, 1)
                        dve.wait_ge(s_dent, jb + 1)
                        for c in range(C):
                            q = jb * C + c
                            num = num_sb[c % 2]
                            dve.wait_ge(s_numc, q + C + 1)
                            dve.wait_ge(s_att, q + 2)
                            chain.step(dve.scalar_tensor_tensor(rec_sb, num, 0.0, num, ALU.is_equal, ALU.add))
                            chain.step(dve.reciprocal(rec_sb, rec_sb))
                            chain.step(dve.tensor_tensor(rec_sb, rec_sb, dent_sb[:, c * CH:(c + 1) * CH], ALU.mult))
                            dve.wait_ge(s_attused, q + 1)
                            dve.scalar_tensor_tensor(att_sb, num, 0.0, rec_sb,
                                                     ALU.not_equal, ALU.mult).then_inc(s_att, 1)
                chain.n = base + T * steps
                for c in range(C):
                    dve.wait_ge(s_y, c + 1)
                    dve.tensor_copy(t_sb[:, c * CH:(c + 1) * CH], psB[:, c * CH:(c + 1) * CH]).then_inc(s_yc, 1)
                for c in range(C):
                    dve.wait_ge(s_yn, c + 1)
                    dve.tensor_copy(h_sb.rearrange("p t f -> p (t f)")[:, c * CH:(c + 1) * CH],
                                    psA[:, c * CH:(c + 1) * CH]).then_inc(s_ync, 1)
                for c in range(C):
                    dve.wait_ge(s_prod, 2 * C + c + 1)
                    dve.tensor_copy(t_sb[:, c * CH:(c + 1) * CH], psB[:, c * CH:(c + 1) * CH]).then_inc(s_t, 1)

        @block.scalar
        def _(act):
            with act.If(act.value_load(b.need_general, min_val=0, max_val=1)):
                act.sem_inc(s_numc, C)
                act.wait_ge(s_var, 1)
                act.activation(stat[:, 2, :], stat[:, 1, :], ACT.Sqrt).then_inc(s_std, 1)
                for layer in range(2):
                    act.wait_ge(s_wh, layer + 1)
                    act.activation(h_sb.rearrange("p t f -> p (t f)"), psB, ACT.Silu).then_inc(s_act, 1)
                act.wait_ge(s_var, 2)
                act.activation(stat[:, 2, :], stat[:, 1, :], ACT.Sqrt).then_inc(s_std, 1)
                with act.Fori(0, T // 2) as i:
                    for half in range(2):
                        jb = 2 * i + half
                        act.wait_ge(s_z, jb + 1)
                        act.activation(den_sb[half], den_sb[half], ACT.Exp).then_inc(s_den, 1)
                        act.wait_ge(s_zt, jb + 1)
                        act.activation(dent_sb, dent_sb, ACT.Exp).then_inc(s_dent, 1)
                        for c in range(C):
                            q = jb * C + c
                            act.wait_ge(s_num, q + 1)
                            act.wait_ge(s_att, q + 1)
                            act.activation(num_sb[c % 2], psA[:, c * CH:(c + 1) * CH], ACT.Copy).then_inc(s_numc, 1)

        @block.tensor
        def _(pe):
            with pe.If(pe.value_load(b.need_general, min_val=0, max_val=1)):
                def propagate(ps, opened):
                    with pe.Fori(0, C) as c:
                        for k in range(T):
                            mm = pe.matmul(ps[:, bass.ds(c * CH, CH)], h_sb[:, k, :], at_sb[:, k, bass.ds(c * CH, CH)],
                                           start=(k == 0 and not opened), stop=(k == T - 1))
                        mm.then_inc(s_prod, 1)

                pe.sem_inc(s_attused, 1)
                pe.sem_inc(s_att, 2)
                pe.wait_ge(s_adj, 16 * T)
                pe.wait_ge(s_h, 1)
                for layer in range(2):
                    if layer == 1:
                        pe.wait_ge(s_act, 1)
                    propagate(psA, False)
                    pe.wait_ge(s_t, (layer + 1) * C)
                    for t in range(T):
                        pe.matmul(psB[:, t * F:(t + 1) * F], t_sb[:, t * P:(t + 1) * P], w0_sb, start=True, stop=False)
                        mm = pe.matmul(psB[:, t * F:(t + 1) * F], ones_sb[0:1, :], b0_sb, start=False, stop=True)
                    mm.then_inc(s_wh, 1)
                pe.wait_ge(s_h, 2)
                for t in range(T):
                    tr = pe.transpose(psA[:, t * P:(t + 1) * P], h_sb[:, t, :], ident)
                    if t % 4 == 3:
                        tr.then_inc(s_hT, 1)
                pe.wait_ge(s_hTc, C)
                for c in range(C):
                    pe.matmul(psB[:, c * CH:(c + 1) * CH], w1_sb, t_sb[:, c * CH:(c + 1) * CH],
                              start=True, stop=True).then_inc(s_xwt, 1)
                for t in range(T):
                    mm = pe.matmul(psA[:, t * F:(t + 1) * F], t_sb[:, t * P:(t + 1) * P], w1_sb, start=True, stop=True)
                mm.then_inc(s_rc, 1)
                pe.wait_ge(s_xwtc, C)
                for t in range(T):
                    mm = pe.matmul(psB[:, 2 * t:2 * t + 2], t_sb[:, t * P:(t + 1) * P], a_sb, start=True, stop=True)
                mm.then_inc(s_rc, 1)
                pe.wait_ge(s_rcc, 2)
                for side, ps in ((0, psA), (1, psB)):
                    for c in range(C):
                        mm = pe.matmul(ps[:, c * CH:(c + 1) * CH], ab_sb[:, side, :], t_sb[:, c * CH:(c + 1) * CH],
                                       start=True, stop=True)
                    mm.then_inc(s_rc, 1)
                pe.wait_ge(s_rcc, 4)
                for c in range(C):
                    pe.matmul(psB[:, c * CH:(c + 1) * CH], zero_sb, at_sb[:, 0, c * CH:(c + 1) * CH],
                              start=True, stop=False)
                with pe.Fori(0, T // 2) as i:
                    for half in range(2):
                        jb = 2 * i + half
                        pe.wait_ge(s_den, jb + 1)
                        for c in range(C):
                            q = jb * C + c
                            pe.wait_ge(s_numc, q + 1)
                            for k in range(T):
                                mm = pe.matmul(psA[:, c * CH:(c + 1) * CH], den_sb[half][:, k, :],
                                               at_sb[:, k, c * CH:(c + 1) * CH], start=(k == 0), stop=(k == T - 1))
                            mm.then_inc(s_num, 1)
                            if c > 0:
                                pe.wait_ge(s_att, q - 1 + 3)
                                pe.matmul(psB[:, (c - 1) * CH:c * CH], xwj_sb[half], att_sb,
                                          start=False, stop=False).then_inc(s_attused, 1)
                        pe.wait_ge(s_att, q + 3)
                        pe.matmul(psB[:, c * CH:(c + 1) * CH], xwj_sb[half], att_sb,
                                  start=False, stop=False).then_inc(s_attused, 1)
                for c in range(C):
                    pe.matmul(psB[:, c * CH:(c + 1) * CH], zero_sb, at_sb[:, 0, c * CH:(c + 1) * CH],
                              start=False, stop=True).then_inc(s_y, 1)
                pe.wait_ge(s_yc, C)
                for t in range(T):
                    tr = pe.transpose(psA[:, t * P:(t + 1) * P], t_sb[:, t * P:(t + 1) * P], ident)
                    if t % 4 == 3:
                        tr.then_inc(s_yn, 1)
                for c in range(C):
                    for t in range(4 * c, 4 * c + 4):
                        pe.matmul(psB[:, t * P:(t + 1) * P], x_sb[:, t, :], ident, start=(t % 4 == 0), stop=False)
                pe.wait_ge(s_ync, C)
                propagate(psB, True)


def build(nc, x, adjT, W0, b0, W1, a1, outT):
    b = buffers(nc, *x.shape)
    build_fast(nc, b, x, adjT, W0, b0, W1, a1, outT)
    build_general(nc, b, x, adjT, outT)


def kernel(x, adj, L0_gnn_W, L0_gnn_b, L1_gnn_W, L1_gnn_a):
    import concourse.bacc as bacc
    from concourse.bass_utils import run_bass_kernel_spmd

    x, adj, W0, b0, W1, a1 = (np.asarray(v) for v in (x, adj, L0_gnn_W, L0_gnn_b, L1_gnn_W, L1_gnn_a))
    F = x.shape[1]
    arrays = {
        "x": x, "adjT": np.ascontiguousarray(adj.T), "W0": W0, "b0": b0.reshape(1, F), "W1": W1,
        "a1": np.ascontiguousarray(a1.reshape(2, F).T),
    }
    nc = bacc.Bacc("TRN2", target_bir_lowering=False, num_devices=1)
    args = [nc.dram_tensor(n, v.shape, mybir.dt.from_np(v.dtype), kind="ExternalInput").ap()
            for n, v in arrays.items()]
    out = nc.dram_tensor("outT", (F, x.shape[0]), FP32, kind="ExternalOutput").ap()
    build(nc, *args, out)
    r = run_bass_kernel_spmd(nc, [arrays], core_ids=[0])
    return np.ascontiguousarray(r.results[0]["outT"].T)
```

```python
import numpy as np
import concourse.bass as bass
import concourse.mybir as mybir

FP32 = mybir.dt.float32
FP32R = mybir.dt.float32r
INT32 = mybir.dt.int32
ALU = mybir.AluOpType
ACT = mybir.ActivationFunctionType
AX = mybir.AxisListType

EPS = 1e-5
SLOPE = 0.01
NO_RANK = 1e6
FAR = 2e4
P = 128
CH = 512
SCORE_LIMIT = 18.0


class Chain:

    def __init__(self, eng, sem):
        self.eng, self.sem, self.n = eng, sem, 0

    def step(self, instruction):
        self.n = self.n + 1
        instruction.then_inc(self.sem, 1)
        self.eng.wait_ge(self.sem, self.n)


class Buffers:
    pass


def buffers(nc, N, F):
    b = Buffers()
    b.N, b.F, b.T, b.C = N, F, N // P, N // CH
    T = b.T
    sb = lambda name, shape, dtype=FP32: nc.alloc_sbuf_tensor(name, shape, dtype).ap()
    b.w0_sb = sb("w0_sb", [F, F])
    b.w1_sb = sb("w1_sb", [F, F])
    b.b0_sb = sb("b0_sb", [1, F])
    b.ones_sb = sb("ones_sb", [P, P])
    b.zero_sb = sb("zero_sb", [P, P])
    b.ident = sb("ident", [P, P])
    b.a_sb = sb("a_sb", [F, 2])
    b.ab_sb = sb("ab_sb", [F, 2, P])
    b.rc_sb = sb("rc_sb", [P, T, 2])
    b.cj_sb = sb("cj_sb", [P, 1])
    b.plan_sb = sb("plan_sb", [P, 2 * P + T + 2])
    b.small = [sb(f"plan{i}", [P, T]) for i in range(3)]
    b.lim_sb = sb("lim_sb", [P, 8])
    b.count_sb = sb("count_sb", [P, 2])
    b.rank_sb = sb("rank_sb", [P, T])
    b.mixed_blocks = sb("mixed_blocks", [P, 1], INT32)[0:1, :]
    b.e_sb = sb("e_sb", [P, T, 2])
    b.cbias = [sb(f"cbias{i}_sb", [P, 2]) for i in range(2)]
    b.xwj_sb = [sb(f"xwj{i}_sb", [P, F]) for i in range(2)]
    b.stat = sb("stat", [P, 4, T])
    b.bn_sb = sb("bn_sb", [P, T, 6])
    b.mv_sb = sb("mv_sb", [P, T, 2])
    b.eps_sb = sb("eps_sb", [P, 1])
    b.odd_sb = sb("odd_sb", [P, T + 1])
    b.guard = sb("guard", [P, 4])
    b.tiny_sb = sb("tiny_sb", [P, 1])
    b.need_general = sb("need_general", [P, 1], INT32)[0:1, :]
    b.go_fast = sb("go_fast", [P, 1], INT32)[0:1, :]
    b.at_off = -(-nc.sbuf_base // 32) * 32
    slot_bytes = 4 * N
    nc.alloc_sbuf_tensor("arena", [P, (T + 9) * N], FP32)
    b.at = lambda name, shape, offset, dtype=FP32: nc.alloc_sbuf_tensor_at(name, shape, dtype, offset=offset).ap()
    b.slot = lambda name, shape, n, part=0, dtype=FP32: b.at(
        name, shape, b.at_off + (T + n) * slot_bytes + part * 4 * CH, dtype)
    b.x_sb = b.slot("x_sb", [P, T, F], 0)
    b.psA = nc.alloc_psum_tensor("psA", [P, N], FP32).ap()
    b.psB = nc.alloc_psum_tensor("psB", [P, N], FP32).ap()
    return b


def build_fast(nc, b, x, adjT, W0, b0, W1, a1, upper, plan, outT):
    N, F, T, C = b.N, b.F, b.T, b.C
    sem = lambda name: nc.alloc_semaphore(name)
    psA, psB, ident, stat, x_sb = b.psA, b.psB, b.ident, b.stat, b.x_sb
    flat = lambda ap: ap.rearrange("p t f -> p (t f)")
    chunk = lambda ap, c: ap[:, c * CH:(c + 1) * CH]

    at_r = b.at("at_r", [P, T, N], b.at_off, FP32R)
    at_raw = b.at("at_raw", [P, T, N], b.at_off)
    raw_last = b.slot("raw_last", [P, N], 5)
    odd = [b.slot(f"odd{i}", [P, N], 6 + i) for i in range(2)]
    hi_r = b.slot("hi_r", [P, T, F], 1, dtype=FP32R)
    lo_r = b.slot("lo_r", [P, T, F], 2, dtype=FP32R)
    t_sb = b.slot("t_sb", [P, N], 3)
    h0_sb = b.slot("h0_sb", [P, T, F], 8)
    h_sb = b.slot("h_sb", [P, T, F], 4)
    h1_sb = b.slot("h1_sb", [P, T, F], 5)
    ht_sb = b.slot("ht_sb", [P, N], 6)
    xwt_sb = b.slot("xwt_sb", [P, N], 3)
    xwc_sb = b.slot("xwc_sb", [P, T, F + 1], 7)
    upper_sb, plan_sb, lim_sb = b.xwj_sb[0], b.plan_sb, b.lim_sb
    sq_sb = b.bn_sb[:, :, 0:2]
    rank_at = plan_sb[:, 0:P]
    block_at = plan_sb[:, P:P + T]
    pair_sb = plan_sb[0:4, P + T:P + T + 2]
    third_sb = plan_sb[0:3, P + T + 2:2 * P + T + 2]
    tail = b.at_off + (T + 8) * 4 * N + 512
    cls_sb = b.at("cls_sb", [P, T, 2], tail)
    u_sb = b.at("u_sb", [P, T, 3], tail + 8 * T)
    w_r = b.at("w_r", [P, T, 4], tail + 20 * T, FP32R)
    none_sb = b.at("none_sb", [P, T, 2], tail + 36 * T)
    cb_sb = b.at("cb_sb", [P, P], tail + 44 * T)
    diag_sb = b.at("diag_sb", [P, P], tail + 44 * T + 4 * P)
    clst_sb = b.at("clst_sb", [P, 2], tail + 44 * T + 12 * P)
    zero_r = b.at("zero_r", [1, P], tail + 44 * T + 12 * P + 32, FP32R)
    one_r = b.at("one_r", [1, P], tail + 44 * T + 16 * P + 32, FP32R)
    b0_hi = b.at("b0_hi", [1, F], tail + 44 * T + 20 * P + 32, FP32R)
    b0_lo = b.at("b0_lo", [1, F], tail + 44 * T + 24 * P + 32, FP32R)
    sum_sb = b.at("sum_sb", [2, F], tail + 44 * T + 8 * P)
    rb01_sb = b.slot("rb01_sb", [P, N], 3)
    sel_sb = b.slot("sel_sb", [P, T, P], 1)
    ut_sb = b.slot("ut_sb", [3, N], 1)
    rb_sb = b.slot("rb_sb", [P, N], 2)
    pt_sb = b.slot("pt_sb", [4, N], 4)
    zt_sb = [b.slot(f"zt{i}_sb", [P, CH], 4, part=i) for i in range(2)]
    att_sb = [b.slot(f"att{i}_sb", [P, CH], 4, part=2 + i) for i in range(2)]
    den_hi = b.slot("den_hi", [P, T, P], 5, dtype=FP32R)
    den_lo = b.slot("den_lo", [P, T, P], 6, dtype=FP32R)
    den_sb = b.slot("den_sb", [P, T, P], 6)
    yt_sb = b.slot("yt_sb", [P, N], 2)
    y_hi = b.slot("y_hi", [P, T, F], 5, dtype=FP32R)
    y_lo = b.slot("y_lo", [P, T, F], 6, dtype=FP32R)
    out_sb = b.slot("out_sb", [P, N], 3)

    s_ld = sem("s_loaded")
    s_x = [sem(f"s_x{c}_loaded") for c in range(C)]
    s_raw = [sem(f"s_tile{t}_loaded") for t in range(T)]
    s_const = sem("s_const")
    s_ident = sem("s_identity_cleared")
    s_ab = sem("s_a_broadcast")
    s_var = sem("s_variance")
    s_std = sem("s_std")
    s_split = sem("s_features_split")
    s_odd = sem("s_odd_terms")
    s_bias = sem("s_bias_split")
    s_ara = sem("s_tile_rounded")
    s_last = sem("s_last_tile_second_half")
    s_bn = sem("s_bn_steps")
    s_scale = sem("s_scales_ready")
    s_ta = sem("s_product_copied_by_act")
    s_hTa = sem("s_transposed_copied_by_act")
    s_xwta = sem("s_xwt_copied_by_act")
    s_prod = sem("s_product_done")
    s_t = sem("s_product_copied")
    s_wh = sem("s_dense_done")
    s_act = sem("s_swish_done")
    s_h = sem("s_normalised")
    s_hd = sem("s_normalised_by_dve")
    s_hT = sem("s_transposed")
    s_hTc = sem("s_transposed_copied")
    s_xwt = sem("s_xwt_done")
    s_xwtc = sem("s_xwt_copied")
    s_rc = sem("s_scores_done")
    s_rcc = sem("s_scores_copied")
    s_xwcc = sem("s_xw_copied")
    s_rng = sem("s_range_terms")
    s_oddall = sem("s_odd_total")
    s_ends = sem("s_row_extremes")
    s_endst = sem("s_extremes_transposed")
    s_endsd = sem("s_extremes_diagonal")
    s_endsb = sem("s_extremes_broadcast")
    s_rows = sem("s_row_totals")
    s_off = sem("s_rank_offsets")
    s_taken = sem("s_columns_taken")
    s_cb = sem("s_columns_copied")
    s_sel = sem("s_selection_ready")
    s_xwc = sem("s_columns_selected")
    s_pc = sem("s_sums_copied")
    s_pn = sem("s_sums_by_node")
    s_cls = sem("s_class_sums")
    s_clst = sem("s_class_sums_transposed")
    s_u = sem("s_u_ready")
    s_ut = sem("s_u_transposed")
    s_utc = sem("s_u_copied")
    s_rb = sem("s_rows_broadcast")
    s_rba = sem("s_rows_copied")
    s_rbd = sem("s_scaled_rows_copied")
    s_rank = sem("s_ranks_ready")
    s_e = sem("s_exp_scores")
    s_w = sem("s_weights_ready")
    s_p = sem("s_sums_done")
    s_diag = sem("s_diagonals")
    s_cbp = sem("s_columns_broadcast")
    s_denfree = sem("s_den_used")
    s_z = sem("s_z_ready")
    s_den = sem("s_den_ready")
    s_denhi = sem("s_den_high_ready")
    s_denlo = sem("s_den_low_ready")
    s_zt = sem("s_zt_ready")
    s_num = sem("s_num_done")
    s_ln = sem("s_ln_ready")
    s_sub = sem("s_logit_ready")
    s_att = sem("s_att_ready")
    s_attused = sem("s_att_used")
    s_y = sem("s_y_done")
    s_yc = sem("s_y_copied")
    s_yn = sem("s_y_nodes")
    s_ync = sem("s_y_nodes_split")
    s_out = sem("s_out")
    s_dve = sem("s_dve_chain")
    s_dve2 = sem("s_dve_chain2")

    x_d = x.rearrange("(t p) f -> p t f", p=P)
    def selection(dve):
        dve.tensor_tensor(sel_sb, rank_at.unsqueeze(1).to_broadcast([P, T, P]),
                          b.rank_sb.unsqueeze(2).to_broadcast([P, T, P]), ALU.is_equal).then_inc(s_sel, 1)

    def select(pe, jb):
        pe.wait_ge(s_sel, jb + 1)
        for t in range(T):
            mm = pe.matmul(psA[:, 0:F + 1], sel_sb[:, t, :], xwc_sb[:, t, :], start=(t == 0), stop=(t == T - 1))
        mm.then_inc(s_xwc, 1)

    def plain_sums(pe, c):
        for k in range(T):
            mm = pe.matmul(psB[0:4, c * CH:(c + 1) * CH], w_r[:, k, :], at_r[:, k, c * CH:(c + 1) * CH],
                           start=(k == 0), stop=(k == T - 1))
        mm.then_inc(s_p, 1)

    with nc.Block() as block:

        @block.sync
        def _(sp):
            for c in range(C):
                part = slice(c * T // C, (c + 1) * T // C)
                sp.dma_start(x_sb[:, part], x_d[:, part]).then_inc(s_x[c], 16)
            for t in range(T):
                sp.dma_start(at_raw[:, t, :] if t < T - 1 else raw_last, adjT[t * P:(t + 1) * P, :]).then_inc(s_raw[t], 16)
                if t == 1:
                    for dst, src in ((b.w0_sb, W0), (b.b0_sb, b0), (b.w1_sb, W1), (b.a_sb, a1),
                                     (upper_sb, upper), (plan_sb, plan)):
                        sp.dma_start(dst, src).then_inc(s_ld, 16)

        @block.gpsimd
        def _(pool):
            pool.memset(b.ones_sb, 1.0).then_inc(s_const, 1)
            pool.memset(b.zero_sb, 0.0).then_inc(s_const, 1)
            pool.memset(b.tiny_sb, 1e-15).then_inc(s_const, 1)
            pool.memset(b.eps_sb, EPS).then_inc(s_const, 1)
            pool.memset(ident, 0.0).then_inc(s_ident, 1)
            pool.wait_ge(s_ident, 1)
            pool.affine_select(out=ident, in_=ident, compare_op=ALU.not_equal, fill=1.0, base=0,
                               pattern=[[-1, P]], channel_multiplier=1).then_inc(s_const, 1)

        @block.vector
        def _(dve):
            chain = Chain(dve, s_dve)

            mean, var = b.mv_sb[:, :, 0], b.mv_sb[:, :, 1]
            std, rstd, shift = (stat[:, i, :] for i in range(3))

            def statistics(turn, c):
                first = (turn * C + c) * 2 * (T // C)
                for t in range(c * T // C, (c + 1) * T // C):
                    dve.bn_stats(b.bn_sb[:, t, :], x_sb[:, t, :]).then_inc(s_bn, 1)
                dve.wait_ge(s_bn, first + T // C)
                for t in range(c * T // C, (c + 1) * T // C):
                    dve.bn_aggr(b.mv_sb[:, t, :], b.bn_sb[:, t, :]).then_inc(s_bn, 1)

            def scales(turn):
                dve.wait_ge(s_std, turn + 1)
                chain.step(dve.reciprocal(rstd, std))
                dve.scalar_tensor_tensor(shift, mean, -1.0, rstd, ALU.mult, ALU.mult).then_inc(s_scale, 1)

            def split(src, part, hi, lo):
                chain.step(dve.tensor_copy(hi[:, part], src[:, part]))
                dve.tensor_tensor(lo[:, part], src[:, part], hi[:, part].bitcast(FP32),
                                  ALU.subtract).then_inc(s_split, 1)

            for c in range(C):
                dve.wait_ge(s_x[c], 16)
                statistics(0, c)
            scales(0)
            for c in range(C):
                dve.wait_ge(s_h, c + 1)
                split(h0_sb, slice(c * T // C, (c + 1) * T // C), hi_r, lo_r)
            dve.wait_ge(s_split, C)
            dve.wait_ge(s_ld, 6 * 16)
            dve.tensor_copy(one_r, b.ones_sb[0:1, :]).then_inc(s_bias, 1)
            chain.step(dve.tensor_copy(b0_hi, b.b0_sb))
            dve.tensor_tensor(b0_lo, b.b0_sb, b0_hi.bitcast(FP32), ALU.subtract).then_inc(s_bias, 1)

            def test(t, tile):
                if t >= 2:
                    dve.wait_ge(s_odd, t - 1)
                dve.scalar_tensor_tensor(odd[t % 2], tile, 0.5, tile, ALU.is_gt,
                                         ALU.not_equal, accum_out=b.odd_sb[:, t:t + 1]).then_inc(s_odd, 1)

            for t in range(T - 1):
                dve.wait_ge(s_raw[t], 16)
                test(t, at_raw[:, t, :])
            dve.wait_ge(s_raw[T - 1], 16)
            dve.tensor_copy(at_r[:, T - 1, N // 2:N], raw_last[:, N // 2:N]).then_inc(s_last, 1)
            dve.wait_ge(s_ld, 6 * 16)
            dve.tensor_copy(b.ab_sb, b.a_sb.unsqueeze(2).to_broadcast([F, 2, P])).then_inc(s_ab, 1)
            for c in range(0, C, 2):
                dve.wait_ge(s_prod, c + 1)
                dve.tensor_copy(chunk(t_sb, c), chunk(psA, c)).then_inc(s_t, 1)
            for c in range(C):
                dve.wait_ge(s_act, c + 1)
                split(h_sb, slice(c * T // C, (c + 1) * T // C), hi_r, lo_r)
            test(T - 1, raw_last)
            dve.wait_ge(s_odd, T)
            for c in range(C + 1):
                if c < C:
                    dve.wait_ge(s_prod, C + c + 1)
                    dve.tensor_copy(chunk(t_sb, c), chunk(psA, c)).then_inc(s_t, 1)
                if c > 0:
                    part = slice((c - 1) * T // C, c * T // C)
                    dve.wait_ge(s_act, C + c)
                    chain.step(dve.tensor_tensor(x_sb[:, part], x_sb[:, part], h_sb[:, part], ALU.add))
                    statistics(1, c - 1)
            scales(1)
            for c in range(0, C, 2):
                for t in range(c * T // C, (c + 1) * T // C):
                    done = dve.tensor_scalar(h1_sb[:, t, :], x_sb[:, t, :], mean[:, t:t + 1], rstd[:, t:t + 1],
                                             ALU.subtract, ALU.mult)
                done.then_inc(s_hd, 1)
            for c in range(0, C, 2):
                dve.wait_ge(s_hT, c + 1)
                dve.tensor_scalar(chunk(ht_sb, c), chunk(psA, c), 0.0, None, ALU.max).then_inc(s_hTc, 1)
            for c in range(0, C, 2):
                dve.wait_ge(s_xwt, c + 1)
                dve.tensor_copy(chunk(xwt_sb, c), chunk(psB, c)).then_inc(s_xwtc, 1)
            dve.wait_ge(s_rc, 1)
            chain.step(dve.tensor_copy(b.rc_sb, psB[:, 0:2 * T].rearrange("p (t o) -> p t o", o=2)))
            dve.tensor_copy(xwc_sb[:, :, F:F + 1], b.rc_sb[:, :, 0:1]).then_inc(s_rcc, 1)
            row, col = b.rc_sb[:, :, 1], b.rc_sb[:, :, 0]
            dve.tensor_reduce(lim_sb[:, 0:1], row, axis=AX.X, op=ALU.max)
            chain.step(dve.tensor_reduce(lim_sb[:, 2:3], row, axis=AX.X, op=ALU.min))
            dve.tensor_scalar(lim_sb[:, 1:2], lim_sb[:, 2:3], -1.0, None, ALU.mult).then_inc(s_ends, 1)
            chain.step(dve.tensor_tensor(sq_sb, b.rc_sb, b.rc_sb, ALU.mult))
            chain.step(dve.tensor_scalar(sq_sb, sq_sb, SCORE_LIMIT ** 2, None, ALU.is_le))
            dve.wait_ge(s_endst, 1)
            chain.step(dve.tensor_reduce(lim_sb[0:2, 2:3], psB[0:2, CH:CH + P], axis=AX.X, op=ALU.max))
            dve.tensor_scalar(lim_sb[0:2, 3:5], ident[0:2, 0:2], lim_sb[0:2, 2:3], None, ALU.mult).then_inc(s_endsd, 1)
            chain.step(dve.tensor_scalar(sq_sb, sq_sb, -1.0, 1.0, ALU.mult, ALU.add))
            dve.tensor_reduce(b.odd_sb[:, T:T + 1], sq_sb, axis=AX.XY, op=ALU.add).then_inc(s_rng, 1)
            dve.wait_ge(s_e, 2)
            chain.step(dve.tensor_copy(w_r[:, :, 0:2], b.e_sb))
            dve.tensor_tensor(w_r[:, :, 2:4], b.e_sb, w_r[:, :, 0:2].bitcast(FP32), ALU.subtract).then_inc(s_w, 1)
            dve.wait_ge(s_endsb, 1)
            chain.step(dve.tensor_copy(lim_sb[:, 5:7], psB[:, CH + P:CH + P + 2]))
            chain.step(dve.tensor_scalar(lim_sb[:, 7:8], lim_sb[:, 5:6], -1.0, None, ALU.mult))
            above, below, mixed, before, ones = cls_sb[:, :, 0], cls_sb[:, :, 1], *b.small
            dve.tensor_scalar(above, col, lim_sb[:, 6:7], None, ALU.is_gt)
            dve.memset(ones, 1.0)
            chain.step(dve.tensor_scalar(below, col, lim_sb[:, 7:8], None, ALU.is_lt))
            chain.step(dve.tensor_tensor(mixed, above, below, ALU.add))
            chain.step(dve.tensor_scalar(mixed, mixed, -1.0, 1.0, ALU.mult, ALU.add))
            chain.step(dve.tensor_tensor_scan(before, ones, mixed, 0.0, ALU.mult, ALU.add))
            dve.tensor_copy(b.count_sb[:, 0:1], before[:, T - 1:T]).then_inc(s_rows, 1)
            dve.wait_ge(s_off, 1)
            chain.step(dve.tensor_copy(b.count_sb, psB[:, CH + P + 2:CH + P + 4]))
            chain.step(dve.tensor_scalar(ones, block_at, b.count_sb[:, 1:2], None, ALU.is_lt))
            chain.step(dve.tensor_reduce(lim_sb[:, 2:3], ones, axis=AX.X, op=ALU.add))
            dve.tensor_copy(b.mixed_blocks, lim_sb[0:1, 2:3])
            chain.step(dve.tensor_tensor(before, before, mixed, ALU.subtract))
            chain.step(dve.tensor_scalar(before, before, b.count_sb[:, 0:1], -NO_RANK, ALU.add, ALU.add))
            chain.step(dve.tensor_tensor(before, before, mixed, ALU.mult))
            chain.step(dve.tensor_scalar(b.rank_sb, before, NO_RANK, None, ALU.add))
            selection(dve)
            g = b.guard
            dve.wait_ge(s_oddall, 1)
            chain.step(dve.tensor_reduce(g[:, 0:1], psB[:, 2 * CH:2 * CH + T + 1], axis=AX.X, op=ALU.add))
            chain.step(dve.tensor_scalar(g[:, 1:2], g[:, 0:1], 0.0, None, ALU.is_le))
            dve.tensor_copy(b.go_fast, g[0:1, 1:2])
            dve.tensor_scalar(b.need_general, g[0:1, 1:2], -1.0, 1.0, ALU.mult, ALU.add)

        @block.scalar
        def _(act):
            def normalise(turn, h):
                act.wait_ge(s_bn, (turn + 1) * 2 * T)
                act.activation(stat[:, 0, :], b.mv_sb[:, :, 1], ACT.Sqrt, bias=b.eps_sb).then_inc(s_std, 1)
                act.wait_ge(s_scale, turn + 1)
                for t in range(T):
                    if turn == 1 and (t * C // T) % 2 == 0:
                        continue
                    done = act.activation(h[:, t, :], x_sb[:, t, :], ACT.Relu, bias=stat[:, 2, t:t + 1],
                                          scale=stat[:, 1, t:t + 1])
                    if t % (T // C) == T // C - 1:
                        done.then_inc(s_h, 1)

            act.wait_ge(s_const, 5)
            normalise(0, h0_sb)
            for t in range(T - 1):
                act.wait_ge(s_odd, t + 1)
                act.activation(at_r[:, t, :], at_raw[:, t, :], ACT.Copy).then_inc(s_ara, 1)
            act.wait_ge(s_raw[T - 1], 16)
            act.activation(at_r[:, T - 1, 0:N // 2], raw_last[:, 0:N // 2], ACT.Copy).then_inc(s_ara, 1)
            for c in range(1, C, 2):
                act.wait_ge(s_prod, c + 1)
                act.activation(chunk(t_sb, c), chunk(psA, c), ACT.Copy).then_inc(s_ta, 1)
            for layer in range(2):
                for c in range(C):
                    act.wait_ge(s_wh, layer * C + c + 1)
                    if layer == 1:
                        act.wait_ge(s_split, C + c + 1)
                    act.activation(chunk(flat(h_sb), c), chunk(psB, c), ACT.Silu).then_inc(s_act, 1)
            normalise(1, h1_sb)
            for c in range(1, C, 2):
                act.wait_ge(s_hT, c + 1)
                act.activation(chunk(ht_sb, c), chunk(psA, c), ACT.Copy).then_inc(s_hTa, 1)
            for c in range(1, C, 2):
                act.wait_ge(s_xwt, c + 1)
                act.activation(chunk(xwt_sb, c), chunk(psB, c), ACT.Copy).then_inc(s_xwta, 1)
            act.preload_act_table_set("natural_log_exp_and_others")
            act.wait_ge(s_rcc, 1)
            act.activation(b.e_sb[:, :, 0:1], b.rc_sb[:, :, 1:2], ACT.Exp).then_inc(s_e, 1)
            act.activation(b.e_sb[:, :, 1:2], b.rc_sb[:, :, 1:2], ACT.Exp, scale=SLOPE).then_inc(s_e, 1)
            for c in range(C):
                act.wait_ge(s_rc, 2 + c)
                act.activation(xwc_sb[:, c * T // C:(c + 1) * T // C, 0:F],
                               chunk(psA, c).rearrange("p (t f) -> p t f", f=F), ACT.Copy).then_inc(s_xwcc, 1)

        @block.tensor
        def _(pe):

            def dense(layer, c):
                bias = lambda part: part.unsqueeze(1).to_broadcast([1, T // C, F])
                pe.matmul(chunk(psB, c), one_r, bias(b0_hi), start=True, stop=False)
                pe.matmul(chunk(psB, c), one_r, bias(b0_lo), start=False, stop=False)
                for t in range(c * T // C, (c + 1) * T // C):
                    mm = pe.matmul(psB[:, t * F:(t + 1) * F], t_sb[:, t * P:(t + 1) * P], b.w0_sb,
                                   start=False, stop=(t == (c + 1) * T // C - 1))
                mm.then_inc(s_wh, 1)

            def product(t, c):
                rhs = at_r[:, t, c * CH:(c + 1) * CH]
                pe.matmul(chunk(psA, c), hi_r[:, t, :], rhs, start=(t == 0), stop=False)
                mm = pe.matmul(chunk(psA, c), lo_r[:, t, :], rhs, start=False, stop=(t == T - 1))
                if t == T - 1:
                    mm.then_inc(s_prod, 1)

            pe.wait_ge(s_const, 5)
            for t in range(T):
                if t % (T // C) == 0:
                    pe.wait_ge(s_split, t // (T // C) + 1)
                pe.wait_ge(s_ara, t + 1)
                for c in range(C):
                    if t == T - 1 and c == C // 2:
                        pe.wait_ge(s_last, 1)
                    product(t, c)
            pe.wait_ge(s_ld, 6 * 16)
            pe.wait_ge(s_bias, 2)
            for c in range(C):
                if c % 2 == 0:
                    pe.wait_ge(s_t, c // 2 + 1)
                else:
                    pe.wait_ge(s_ta, c // 2 + 1)
                dense(0, c)
            for c in range(C):
                for t in range(T):
                    if c == 0 and t % (T // C) == 0:
                        pe.wait_ge(s_split, C + t // (T // C) + 1)
                    product(t, c)
                if c > 0:
                    pe.wait_ge(s_t, C // 2 + c)
                    dense(1, c - 1)
            pe.wait_ge(s_t, C // 2 + C)
            dense(1, C - 1)
            for t in range(T):
                if t % (T // C) == 0:
                    c = t // (T // C)
                    if c % 2 == 0:
                        pe.wait_ge(s_hd, c // 2 + 1)
                    else:
                        pe.wait_ge(s_h, C + c // 2 + 1)
                tr = pe.transpose(psA[:, t * P:(t + 1) * P], h1_sb[:, t, :], ident)
                if t % 4 == 3:
                    tr.then_inc(s_hT, 1)
            for c in range(C):
                if c % 2 == 0:
                    pe.wait_ge(s_hTc, c // 2 + 1)
                else:
                    pe.wait_ge(s_hTa, c // 2 + 1)
                pe.matmul(chunk(psB, c), b.w1_sb, chunk(ht_sb, c), start=True, stop=True).then_inc(s_xwt, 1)
            pe.wait_ge(s_ab, 1)
            for t in range(T):
                if t % (T // C) == 0:
                    c = t // (T // C)
                    if c % 2 == 0:
                        pe.wait_ge(s_xwtc, c // 2 + 1)
                    else:
                        pe.wait_ge(s_xwta, c // 2 + 1)
                mm = pe.matmul(psB[:, 2 * t:2 * t + 2], xwt_sb[:, t * P:(t + 1) * P], b.a_sb, start=True, stop=True)
            mm.then_inc(s_rc, 1)

            def xw(c):
                for t in range(c * T // C, (c + 1) * T // C):
                    mm = pe.matmul(psA[:, t * F:(t + 1) * F], ht_sb[:, t * P:(t + 1) * P], b.w1_sb,
                                   start=True, stop=True)
                mm.then_inc(s_rc, 1)

            xw(0)
            pe.wait_ge(s_ends, 1)
            pe.transpose(psB[0:2, CH:CH + P], lim_sb[:, 0:2], ident).then_inc(s_endst, 1)
            xw(1)
            pe.wait_ge(s_endsd, 1)
            pe.matmul(psB[:, CH + P:CH + P + 2], b.ones_sb[0:2, :], lim_sb[0:2, 3:5],
                      start=True, stop=True).then_inc(s_endsb, 1)
            xw(2)
            xw(3)
            pe.wait_ge(s_rng, 1)
            pe.matmul(psB[:, 2 * CH:2 * CH + T + 1], b.ones_sb, b.odd_sb, start=True, stop=True).then_inc(s_oddall, 1)
            pe.wait_ge(s_rows, 1)
            pe.matmul(psB[:, CH + P + 2:CH + P + 3], upper_sb, b.count_sb[:, 0:1], start=True, stop=True)
            pe.matmul(psB[:, CH + P + 3:CH + P + 4], b.ones_sb, b.count_sb[:, 0:1],
                      start=True, stop=True).then_inc(s_off, 1)
            pe.wait_ge(s_xwcc, C)
            for t in range(T):
                mm = pe.matmul(psA[:, 3 * CH:3 * CH + 2], xwc_sb[:, t, 0:F], cls_sb[:, t, :], start=(t == 0), stop=(t == T - 1))
            mm.then_inc(s_cls, 1)
            pe.wait_ge(s_w, 1)
            plain_sums(pe, 0)
            select(pe, 0)

    with nc.Block() as block:

        @block.sync
        def _(sp):
            with sp.If(sp.value_load(b.go_fast, min_val=0, max_val=1)):
                for c in range(C):
                    sp.wait_ge(s_t, C // 2 + C + c + 1)
                    sp.dma_start(chunk(outT, c), chunk(out_sb, c)).then_inc(s_out, 16)
                sp.wait_ge(s_out, 16 * C)

        @block.vector
        def _(dve):
            with dve.If(dve.value_load(b.go_fast, min_val=0, max_val=1)):
                chain = Chain(dve, s_dve2)
                mixed_blocks = dve.value_load(b.mixed_blocks, min_val=0, max_val=T)
                Q = T // 4

                def take(jb, half):
                    dve.wait_ge(s_xwc, jb + 1)
                    dve.tensor_copy(b.xwj_sb[half], psA[:, 0:F]).then_inc(s_taken, 1)
                    dve.tensor_scalar(b.cbias[half][:, 0:1], psA[:, F:F + 1], 1.0 - SLOPE, None,
                                      ALU.mult).then_inc(s_taken, 1)
                    dve.tensor_scalar(b.cbias[half][:, 1:2], psA[:, F:F + 1], SLOPE, None, ALU.mult).then_inc(s_taken, 1)
                    dve.tensor_copy(b.cj_sb, psA[:, F:F + 1]).then_inc(s_taken, 1)
                    dve.wait_ge(s_taken, 4 * jb + 4)
                    dve.tensor_scalar(diag_sb, ident, b.cj_sb, None, ALU.mult).then_inc(s_diag, 1)

                def columns(jb):
                    dve.wait_ge(s_cbp, jb + 1)
                    dve.tensor_copy(cb_sb, psA[:, F + P:F + 2 * P]).then_inc(s_cb, 1)

                def scores(jb, qd):
                    part = slice(qd * Q, (qd + 1) * Q)
                    dve.wait_ge(s_cb, jb + 1)
                    if qd < 3:
                        dve.wait_ge(s_denfree, 3 * jb + qd + 1)
                    else:
                        dve.wait_ge(s_num, jb * C + C * C)
                    cols = cb_sb.unsqueeze(1).to_broadcast([P, Q, P])
                    rows = b.rc_sb[:, part, 1:2].to_broadcast([P, Q, P])
                    dve.tensor_tensor(den_sb[:, part], cols, rows, ALU.add).then_inc(s_z, 1)
                    dve.wait_ge(s_z, 8 * jb + 2 * qd + 1)
                    dve.scalar_tensor_tensor(den_sb[:, part], den_sb[:, part], SLOPE, den_sb[:, part],
                                             ALU.mult, ALU.max).then_inc(s_z, 1)

                def low(jb, qd):
                    part = slice(qd * Q, (qd + 1) * Q)
                    dve.wait_ge(s_denhi, 4 * jb + qd + 1)
                    dve.tensor_tensor(den_lo[:, part], den_sb[:, part], den_hi[:, part].bitcast(FP32),
                                      ALU.subtract).then_inc(s_denlo, 1)

                def den_first(jb):
                    scores(jb, 0)
                    scores(jb, 1)
                    low(jb, 0)
                    scores(jb, 2)
                    low(jb, 1)

                def den_last(jb):
                    low(jb, 2)
                    scores(jb, 3)
                    low(jb, 3)

                def block(jb, half):
                    for c in range(C):
                        q = jb * C + c
                        if c == 3:
                            with dve.If(mixed_blocks > jb + 1):
                                den_first(jb + 1)
                                den_last(jb + 1)
                        dve.wait_ge(s_sub, q - 1 + C)
                        dve.scalar_tensor_tensor(zt_sb[c % 2], chunk(rb_sb, c), b.cbias[half][:, 0:1],
                                                 chunk(rb01_sb, c), ALU.add, ALU.max).then_inc(s_zt, 1)
                        dve.wait_ge(s_attused, q - 1 + 2 * C)
                        dve.wait_ge(s_zt, q + 1)
                        dve.wait_ge(s_ln, q + 1)
                        dve.tensor_tensor(att_sb[c % 2], zt_sb[c % 2], chunk(psA, c),
                                          ALU.subtract).then_inc(s_sub, 1)
                        if c == 0:
                            with dve.If(mixed_blocks > jb + 1):
                                dve.tensor_scalar(b.rank_sb, b.rank_sb, -float(P), None, ALU.add).then_inc(s_rank, 1)
                                dve.wait_ge(s_rank, jb + 1)
                                selection(dve)
                        if c == 1:
                            with dve.If(mixed_blocks > jb + 1):
                                take(jb + 1, 1 - half)
                        if c == 2:
                            with dve.If(mixed_blocks > jb + 1):
                                columns(jb + 1)

                dve.tensor_copy(zero_r, b.zero_sb[0:1, :])
                dve.tensor_copy(clst_sb, psA[:, 3 * CH:3 * CH + 2]).then_inc(s_cls, 1)
                take(0, 0)
                columns(0)
                with dve.If(mixed_blocks > 0):
                    den_first(0)
                dve.wait_ge(s_clst, 1)
                dve.wait_ge(s_pn, T)
                dve.tensor_copy(sum_sb, psA[0:2, 3 * CH + F:3 * CH + 2 * F]).then_inc(s_u, 1)
                sums = psA[:, 2 * CH:2 * CH + 2 * T].rearrange("p (t o) -> p t o", o=2)
                chain.step(dve.tensor_scalar(none_sb, sums, 0.0, None, ALU.is_le))
                chain.step(dve.tensor_tensor(u_sb[:, :, 0:2], sums, none_sb, ALU.add))
                chain.step(dve.reciprocal(u_sb[:, :, 0:2], u_sb[:, :, 0:2]))
                chain.step(dve.tensor_tensor(u_sb[:, :, 0:2], u_sb[:, :, 0:2], b.e_sb, ALU.mult))
                chain.step(dve.scalar_tensor_tensor(u_sb[:, :, 0:2], none_sb, 0.0, u_sb[:, :, 0:2],
                                                    ALU.is_equal, ALU.mult))
                dve.scalar_tensor_tensor(u_sb[:, :, 2:3], none_sb[:, :, 0:1], -FAR, b.rc_sb[:, :, 1:2],
                                         ALU.mult, ALU.add).then_inc(s_u, 1)
                with dve.If(mixed_blocks > 0):
                    den_last(0)
                for c in range(C):
                    dve.wait_ge(s_rba, c + 1)
                    dve.tensor_scalar(chunk(rb01_sb, c), chunk(rb_sb, c), SLOPE, None, ALU.mult).then_inc(s_rbd, 1)
                dve.wait_ge(s_rbd, C)
                with dve.Fori(0, T // 4) as g:
                    with dve.If(mixed_blocks > 4 * g):
                        with dve.Fori(0, 2) as i:
                            for half in range(2):
                                with dve.If(mixed_blocks > 4 * g + 2 * i + half):
                                    block(4 * g + 2 * i + half, half)
                for c in range(C):
                    dve.wait_ge(s_y, c + 1)
                    dve.tensor_copy(chunk(yt_sb, c), chunk(psB, c)).then_inc(s_yc, 1)
                for c in range(C):
                    dve.wait_ge(s_yn, c + 1)
                    part = slice(c * T // C, (c + 1) * T // C)
                    chain.step(dve.tensor_copy(flat(y_hi[:, part]), chunk(psA, c)))
                    dve.tensor_tensor(flat(y_lo[:, part]), chunk(psA, c), flat(y_hi[:, part].bitcast(FP32)),
                                      ALU.subtract).then_inc(s_ync, 1)
                for c in range(C):
                    dve.wait_ge(s_prod, 2 * C + c + 1)
                    dve.tensor_copy(chunk(out_sb, c), chunk(psB, c)).then_inc(s_t, 1)

        @block.scalar
        def _(act):
            with act.If(act.value_load(b.go_fast, min_val=0, max_val=1)):
                mixed_blocks = act.value_load(b.mixed_blocks, min_val=0, max_val=T)
                Q = T // 4

                def den_exp(jb, qd):
                    part = slice(qd * Q, (qd + 1) * Q)
                    act.wait_ge(s_z, 8 * jb + 2 * qd + 2)
                    act.activation(den_sb[:, part], den_sb[:, part], ACT.Exp).then_inc(s_den, 1)
                    act.wait_ge(s_den, 4 * jb + qd + 1)
                    act.activation(den_hi[:, part], den_sb[:, part], ACT.Copy).then_inc(s_denhi, 1)

                def block(jb, half):
                    for c in range(C):
                        q = jb * C + c
                        if c == 3:
                            with act.If(mixed_blocks > jb + 1):
                                for qd in range(4):
                                    den_exp(jb + 1, qd)
                        act.wait_ge(s_num, q + C * C + 1)
                        act.activation(chunk(psA, c), chunk(psA, c), ACT.Ln, bias=b.tiny_sb).then_inc(s_ln, 1)
                        act.wait_ge(s_sub, q + 1 + C)
                        act.activation(att_sb[c % 2], att_sb[c % 2], ACT.Exp,
                                       bias=b.cbias[half][:, 1:2]).then_inc(s_att, 1)

                for c in range(C):
                    act.wait_ge(s_p, c + 1)
                    act.activation(chunk(pt_sb, c), psB[0:4, c * CH:(c + 1) * CH], ACT.Copy).then_inc(s_pc, 1)
                    if c > 0:
                        with act.If(mixed_blocks > 0):
                            den_exp(0, c - 1)
                for c in range(C):
                    act.wait_ge(s_ut, c + 1)
                    act.activation(chunk(ut_sb, c), psB[0:3, c * CH:(c + 1) * CH], ACT.Copy).then_inc(s_utc, 1)
                with act.If(mixed_blocks > 0):
                    den_exp(0, 3)
                for c in range(C):
                    act.wait_ge(s_rb, c + 1)
                    act.activation(chunk(rb_sb, c), chunk(psB, c), ACT.Copy).then_inc(s_rba, 1)
                with act.Fori(0, T // 4) as g:
                    with act.If(mixed_blocks > 4 * g):
                        with act.Fori(0, 2) as i:
                            for half in range(2):
                                with act.If(mixed_blocks > 4 * g + 2 * i + half):
                                    block(4 * g + 2 * i + half, half)

        @block.tensor
        def _(pe):
            with pe.If(pe.value_load(b.go_fast, min_val=0, max_val=1)):
                mixed_blocks = pe.value_load(b.mixed_blocks, min_val=0, max_val=T)
                pe.sem_inc(s_num, C * C)
                pe.sem_inc(s_denfree, 3)
                pe.sem_inc(s_attused, 2 * C)
                pe.sem_inc(s_sub, C)
                pe.sem_inc(s_att, C)

                def broadcast(jb):
                    pe.wait_ge(s_diag, jb + 1)
                    pe.matmul(psA[:, F + P:F + 2 * P], b.ones_sb, diag_sb, start=True, stop=True).then_inc(s_cbp, 1)

                def use(jb, half, c, before=0):
                    pe.wait_ge(s_att, (jb + 1 - before) * C + c + 1)
                    pe.matmul(chunk(psB, c), b.xwj_sb[half], att_sb[c % 2],
                              start=False, stop=False).then_inc(s_attused, 1)

                def block(jb, half):
                    for c in range(C):
                        pe.wait_ge(s_sub, jb * C + c + 1)
                        for k in range(T):
                            if c == 0 and k % 4 == 0:
                                pe.wait_ge(s_denlo, 4 * jb + k // 4 + 1)
                            rhs = at_r[:, k, c * CH:(c + 1) * CH]
                            pe.matmul(chunk(psA, c), den_hi[:, k, :], rhs, start=(k == 0), stop=False)
                            mm = pe.matmul(chunk(psA, c), den_lo[:, k, :], rhs, start=False, stop=(k == T - 1))
                            if c == C - 1 and k % 4 == 3 and k < T - 1:
                                mm.then_inc(s_denfree, 1)
                        mm.then_inc(s_num, 1)
                        if c > 0:
                            use(jb, half, c - 1)
                        else:
                            with pe.If(jb > 0):
                                use(jb, 1 - half, C - 1, 1)
                        if c == 1:
                            with pe.If(mixed_blocks > jb + 1):
                                pe.wait_ge(s_sub, (jb + 1) * C + 1)
                                select(pe, jb + 1)
                        if c == 2:
                            with pe.If(mixed_blocks > jb + 1):
                                broadcast(jb + 1)
                    with pe.If(mixed_blocks < jb + 2):
                        use(jb, half, C - 1)

                def by_node(c):
                    pe.wait_ge(s_pc, c + 1)
                    for t in range(c * T // C, (c + 1) * T // C):
                        pe.matmul(psA[:, 2 * CH + 2 * t:2 * CH + 2 * t + 2], pt_sb[:, t * P:(t + 1) * P], pair_sb,
                                  start=True, stop=True).then_inc(s_pn, 1)

                plain_sums(pe, 1)
                by_node(0)
                broadcast(0)
                plain_sums(pe, 2)
                by_node(1)
                plain_sums(pe, 3)
                by_node(2)
                pe.wait_ge(s_cls, 2)
                pe.transpose(psA[0:2, 3 * CH + F:3 * CH + 2 * F], clst_sb, ident).then_inc(s_clst, 1)
                by_node(3)
                pe.wait_ge(s_u, 2)
                for t in range(T):
                    tr = pe.transpose(psB[0:3, t * P:(t + 1) * P], u_sb[:, t, :], ident)
                    if t % 4 == 3:
                        tr.then_inc(s_ut, 1)
                for c in range(C):
                    pe.wait_ge(s_utc, c + 1)
                    pe.matmul(chunk(psB, c), third_sb, chunk(ut_sb, c), start=True, stop=True).then_inc(s_rb, 1)
                for c in range(C):
                    pe.wait_ge(s_rba, c + 1)
                    pe.matmul(chunk(psB, c), sum_sb, ut_sb[0:2, c * CH:(c + 1) * CH], start=True, stop=False)
                with pe.Fori(0, T // 4) as g:
                    with pe.If(mixed_blocks > 4 * g):
                        with pe.Fori(0, 2) as i:
                            for half in range(2):
                                with pe.If(mixed_blocks > 4 * g + 2 * i + half):
                                    block(4 * g + 2 * i + half, half)
                for c in range(C):
                    pe.matmul(chunk(psB, c), zero_r, at_r[0:1, 0, c * CH:(c + 1) * CH],
                              start=False, stop=True).then_inc(s_y, 1)
                for c in range(C):
                    pe.wait_ge(s_yc, c + 1)
                    for t in range(4 * c, 4 * c + 4):
                        tr = pe.transpose(psA[:, t * P:(t + 1) * P], yt_sb[:, t * P:(t + 1) * P], ident)
                    tr.then_inc(s_yn, 1)
                for c in range(C):
                    for t in range(4 * c, 4 * c + 4):
                        pe.matmul(psB[:, t * P:(t + 1) * P], x_sb[:, t, :], ident, start=(t % 4 == 0), stop=False)
                    for t in range(T):
                        if c == 0 and t % 4 == 0:
                            pe.wait_ge(s_ync, t // 4 + 1)
                        rhs = at_r[:, t, c * CH:(c + 1) * CH]
                        pe.matmul(chunk(psB, c), y_hi[:, t, :], rhs, start=False, stop=False)
                        mm = pe.matmul(chunk(psB, c), y_lo[:, t, :], rhs, start=False, stop=(t == T - 1))
                    mm.then_inc(s_prod, 1)


def build_general(nc, b, x, adjT, outT):
    N, F, T, C = b.N, b.F, b.T, b.C
    sem = lambda name: nc.alloc_semaphore("g_" + name)
    at_sb = b.at("g_at_sb", [P, T, N], b.at_off)
    x_sb = b.x_sb
    h_sb = b.slot("g_h_sb", [P, T, F], 1)
    t_sb = b.slot("g_t_sb", [P, N], 2)
    cb_sb = b.slot("g_cb_sb", [P, N], 3)
    rb_sb = b.slot("g_rb_sb", [P, N], 4)
    den_sb = [b.slot(f"g_den{i}_sb", [P, T, P], 5 + i) for i in range(2)]
    dent_sb = b.slot("g_dent_sb", [P, N], 7)
    num_sb = [b.slot(f"g_num{i}_sb", [P, CH], 8, part=i) for i in range(2)]
    rec_sb = b.slot("g_rec_sb", [P, CH], 8, part=2)
    att_sb = b.slot("g_att_sb", [P, CH], 8, part=3)
    w0_sb, w1_sb, b0_sb, ones_sb, zero_sb, a_sb, ab_sb, rc_sb, cj_sb, ident, stat, xwj_sb = (
        b.w0_sb, b.w1_sb, b.b0_sb, b.ones_sb, b.zero_sb, b.a_sb, b.ab_sb, b.rc_sb, b.cj_sb, b.ident, b.stat, b.xwj_sb)
    psA, psB = b.psA, b.psB
    s_ld = sem("s_loaded")
    s_adj = sem("s_adj_loaded")
    s_var = sem("s_variance")
    s_std = sem("s_std")
    s_h = sem("s_features_ready")
    s_prod = sem("s_product_done")
    s_t = sem("s_product_copied")
    s_wh = sem("s_dense_done")
    s_act = sem("s_swish_done")
    s_hT = sem("s_transposed")
    s_hTc = sem("s_transposed_copied")
    s_xwt = sem("s_xwt_done")
    s_xwtc = sem("s_xwt_copied")
    s_rc = sem("s_scores_done")
    s_rcc = sem("s_scores_copied")
    s_z = sem("s_z_ready")
    s_den = sem("s_den_ready")
    s_zt = sem("s_zt_ready")
    s_dent = sem("s_dent_ready")
    s_num = sem("s_num_done")
    s_numc = sem("s_num_copied")
    s_safe = sem("s_num_read")
    s_att = sem("s_att_ready")
    s_attused = sem("s_att_used")
    s_y = sem("s_y_done")
    s_yc = sem("s_y_copied")
    s_yn = sem("s_y_nodes")
    s_ync = sem("s_y_nodes_copied")
    s_out = sem("s_out")
    s_dve = sem("s_dve_chain")

    x_d = x.rearrange("(t p) f -> p t f", p=P)
    at_d = adjT.rearrange("(t p) n -> p t n", p=P)

    with nc.Block() as block:

        @block.sync
        def _(sp):
            with sp.If(sp.value_load(b.need_general, min_val=0, max_val=1)):
                sp.dma_start(x_sb, x_d).then_inc(s_ld, 16)
                for t in range(T):
                    sp.dma_start(at_sb[:, t, :], at_d[:, t, :]).then_inc(s_adj, 16)
                for c in range(C):
                    sp.wait_ge(s_t, 2 * C + c + 1)
                    sp.dma_start(outT[:, c * CH:(c + 1) * CH], t_sb[:, c * CH:(c + 1) * CH]).then_inc(s_out, 16)
                sp.wait_ge(s_out, 16 * C)

        @block.vector
        def _(dve):
            with dve.If(dve.value_load(b.need_general, min_val=0, max_val=1)):
                chain = Chain(dve, s_dve)

                def layernorm_relu(turn):
                    mean, var, std, rstd = (stat[:, i, :] for i in range(4))
                    chain.step(dve.tensor_reduce(mean, x_sb, axis=AX.X, op=ALU.add))
                    chain.step(dve.tensor_scalar(mean, mean, 1.0 / F, None, ALU.mult))
                    chain.step(dve.tensor_tensor(x_c, x_sb, mean.unsqueeze(2).to_broadcast([P, T, F]), ALU.subtract))
                    chain.step(dve.tensor_tensor(h_sb, x_c, x_c, ALU.mult))
                    chain.step(dve.tensor_reduce(var, h_sb, axis=AX.X, op=ALU.add))
                    dve.tensor_scalar(var, var, 1.0 / F, EPS, ALU.mult, ALU.add).then_inc(s_var, 1)
                    dve.wait_ge(s_std, turn + 1)
                    chain.step(dve.reciprocal(rstd, std))
                    dve.scalar_tensor_tensor(h_sb, x_c, 0.0, rstd.unsqueeze(2).to_broadcast([P, T, F]),
                                             ALU.max, ALU.mult).then_inc(s_h, 1)

                x_c = dent_sb.rearrange("p (t f) -> p t f", f=F)
                dve.wait_ge(s_ld, 16)
                layernorm_relu(0)
                for layer in range(2):
                    for c in range(C):
                        dve.wait_ge(s_prod, layer * C + c + 1)
                        dve.tensor_copy(t_sb[:, c * CH:(c + 1) * CH], psA[:, c * CH:(c + 1) * CH]).then_inc(s_t, 1)
                dve.wait_ge(s_act, 2)
                chain.step(dve.tensor_tensor(x_sb, x_sb, h_sb, ALU.add))
                layernorm_relu(1)
                for c in range(C):
                    dve.wait_ge(s_hT, c + 1)
                    dve.tensor_copy(t_sb[:, c * CH:(c + 1) * CH], psA[:, c * CH:(c + 1) * CH]).then_inc(s_hTc, 1)
                dve.wait_ge(s_rc, 1)
                for c in range(C):
                    dve.wait_ge(s_xwt, c + 1)
                    dve.tensor_copy(t_sb[:, c * CH:(c + 1) * CH], psB[:, c * CH:(c + 1) * CH]).then_inc(s_xwtc, 1)
                dve.wait_ge(s_rc, 1)
                dve.tensor_copy(h_sb, psA.rearrange("p (t f) -> p t f", f=F)).then_inc(s_rcc, 1)
                dve.wait_ge(s_rc, 2)
                dve.tensor_copy(rc_sb, psB[:, 0:2 * T].rearrange("p (t o) -> p t o", o=2)).then_inc(s_rcc, 1)
                dve.wait_ge(s_rc, 3)
                dve.tensor_copy(cb_sb, psA).then_inc(s_rcc, 1)
                dve.wait_ge(s_rc, 4)
                chain.step(dve.tensor_copy(rb_sb, psB))
                dve.sem_inc(s_rcc, 1)

                base = chain.n
                steps = 5 + 3 * C
                with dve.Fori(0, T // 2) as i:
                    for half in range(2):
                        jb = 2 * i + half
                        chain.n = base + jb * steps
                        cols = cb_sb[:, bass.ds(jb * P, P)].unsqueeze(1).to_broadcast([P, T, P])
                        rows = rc_sb[:, :, 1:2].to_broadcast([P, T, P])
                        chain.step(dve.tensor_tensor(den_sb[half], cols, rows, ALU.add))
                        dve.scalar_tensor_tensor(den_sb[half], den_sb[half], SLOPE, den_sb[half],
                                                 ALU.mult, ALU.max).then_inc(s_z, 1)
                        chain.step(dve.tensor_copy(cj_sb, rc_sb[:, bass.ds(jb, 1), 0]))
                        chain.step(dve.tensor_copy(xwj_sb[half], h_sb[:, bass.ds(jb, 1), :].squeeze(1)))
                        chain.step(dve.tensor_scalar(dent_sb, rb_sb, cj_sb, None, ALU.add))
                        chain.step(dve.scalar_tensor_tensor(dent_sb, dent_sb, SLOPE, dent_sb, ALU.mult, ALU.max))
                        dve.sem_inc(s_zt, 1)
                        dve.wait_ge(s_dent, jb + 1)
                        for c in range(C):
                            q = jb * C + c
                            num = num_sb[c % 2]
                            dve.wait_ge(s_numc, q + C + 1)
                            dve.wait_ge(s_att, q + 2)
                            chain.step(dve.scalar_tensor_tensor(rec_sb, num, 0.0, num, ALU.is_equal, ALU.add))
                            chain.step(dve.reciprocal(rec_sb, rec_sb))
                            chain.step(dve.tensor_tensor(rec_sb, rec_sb, dent_sb[:, c * CH:(c + 1) * CH], ALU.mult))
                            dve.wait_ge(s_attused, q + 1)
                            dve.scalar_tensor_tensor(att_sb, num, 0.0, rec_sb,
                                                     ALU.not_equal, ALU.mult).then_inc(s_att, 1)
                chain.n = base + T * steps
                for c in range(C):
                    dve.wait_ge(s_y, c + 1)
                    dve.tensor_copy(t_sb[:, c * CH:(c + 1) * CH], psB[:, c * CH:(c + 1) * CH]).then_inc(s_yc, 1)
                for c in range(C):
                    dve.wait_ge(s_yn, c + 1)
                    dve.tensor_copy(h_sb.rearrange("p t f -> p (t f)")[:, c * CH:(c + 1) * CH],
                                    psA[:, c * CH:(c + 1) * CH]).then_inc(s_ync, 1)
                for c in range(C):
                    dve.wait_ge(s_prod, 2 * C + c + 1)
                    dve.tensor_copy(t_sb[:, c * CH:(c + 1) * CH], psB[:, c * CH:(c + 1) * CH]).then_inc(s_t, 1)

        @block.scalar
        def _(act):
            with act.If(act.value_load(b.need_general, min_val=0, max_val=1)):
                act.sem_inc(s_numc, C)
                act.wait_ge(s_var, 1)
                act.activation(stat[:, 2, :], stat[:, 1, :], ACT.Sqrt).then_inc(s_std, 1)
                for layer in range(2):
                    act.wait_ge(s_wh, layer + 1)
                    act.activation(h_sb.rearrange("p t f -> p (t f)"), psB, ACT.Silu).then_inc(s_act, 1)
                act.wait_ge(s_var, 2)
                act.activation(stat[:, 2, :], stat[:, 1, :], ACT.Sqrt).then_inc(s_std, 1)
                with act.Fori(0, T // 2) as i:
                    for half in range(2):
                        jb = 2 * i + half
                        act.wait_ge(s_z, jb + 1)
                        act.activation(den_sb[half], den_sb[half], ACT.Exp).then_inc(s_den, 1)
                        act.wait_ge(s_zt, jb + 1)
                        act.activation(dent_sb, dent_sb, ACT.Exp).then_inc(s_dent, 1)
                        for c in range(C):
                            q = jb * C + c
                            act.wait_ge(s_num, q + 1)
                            act.wait_ge(s_att, q + 1)
                            act.activation(num_sb[c % 2], psA[:, c * CH:(c + 1) * CH], ACT.Copy).then_inc(s_numc, 1)

        @block.tensor
        def _(pe):
            with pe.If(pe.value_load(b.need_general, min_val=0, max_val=1)):
                def propagate(ps, opened):
                    with pe.Fori(0, C) as c:
                        for k in range(T):
                            mm = pe.matmul(ps[:, bass.ds(c * CH, CH)], h_sb[:, k, :], at_sb[:, k, bass.ds(c * CH, CH)],
                                           start=(k == 0 and not opened), stop=(k == T - 1))
                        mm.then_inc(s_prod, 1)

                pe.sem_inc(s_attused, 1)
                pe.sem_inc(s_att, 2)
                pe.wait_ge(s_adj, 16 * T)
                pe.wait_ge(s_h, 1)
                for layer in range(2):
                    if layer == 1:
                        pe.wait_ge(s_act, 1)
                    propagate(psA, False)
                    pe.wait_ge(s_t, (layer + 1) * C)
                    for t in range(T):
                        pe.matmul(psB[:, t * F:(t + 1) * F], t_sb[:, t * P:(t + 1) * P], w0_sb, start=True, stop=False)
                        mm = pe.matmul(psB[:, t * F:(t + 1) * F], ones_sb[0:1, :], b0_sb, start=False, stop=True)
                    mm.then_inc(s_wh, 1)
                pe.wait_ge(s_h, 2)
                for t in range(T):
                    tr = pe.transpose(psA[:, t * P:(t + 1) * P], h_sb[:, t, :], ident)
                    if t % 4 == 3:
                        tr.then_inc(s_hT, 1)
                pe.wait_ge(s_hTc, C)
                for c in range(C):
                    pe.matmul(psB[:, c * CH:(c + 1) * CH], w1_sb, t_sb[:, c * CH:(c + 1) * CH],
                              start=True, stop=True).then_inc(s_xwt, 1)
                for t in range(T):
                    mm = pe.matmul(psA[:, t * F:(t + 1) * F], t_sb[:, t * P:(t + 1) * P], w1_sb, start=True, stop=True)
                mm.then_inc(s_rc, 1)
                pe.wait_ge(s_xwtc, C)
                for t in range(T):
                    mm = pe.matmul(psB[:, 2 * t:2 * t + 2], t_sb[:, t * P:(t + 1) * P], a_sb, start=True, stop=True)
                mm.then_inc(s_rc, 1)
                pe.wait_ge(s_rcc, 2)
                for side, ps in ((0, psA), (1, psB)):
                    for c in range(C):
                        mm = pe.matmul(ps[:, c * CH:(c + 1) * CH], ab_sb[:, side, :], t_sb[:, c * CH:(c + 1) * CH],
                                       start=True, stop=True)
                    mm.then_inc(s_rc, 1)
                pe.wait_ge(s_rcc, 4)
                for c in range(C):
                    pe.matmul(psB[:, c * CH:(c + 1) * CH], zero_sb, at_sb[:, 0, c * CH:(c + 1) * CH],
                              start=True, stop=False)
                with pe.Fori(0, T // 2) as i:
                    for half in range(2):
                        jb = 2 * i + half
                        pe.wait_ge(s_den, jb + 1)
                        for c in range(C):
                            q = jb * C + c
                            pe.wait_ge(s_numc, q + 1)
                            for k in range(T):
                                mm = pe.matmul(psA[:, c * CH:(c + 1) * CH], den_sb[half][:, k, :],
                                               at_sb[:, k, c * CH:(c + 1) * CH], start=(k == 0), stop=(k == T - 1))
                            mm.then_inc(s_num, 1)
                            if c > 0:
                                pe.wait_ge(s_att, q - 1 + 3)
                                pe.matmul(psB[:, (c - 1) * CH:c * CH], xwj_sb[half], att_sb,
                                          start=False, stop=False).then_inc(s_attused, 1)
                        pe.wait_ge(s_att, q + 3)
                        pe.matmul(psB[:, c * CH:(c + 1) * CH], xwj_sb[half], att_sb,
                                  start=False, stop=False).then_inc(s_attused, 1)
                for c in range(C):
                    pe.matmul(psB[:, c * CH:(c + 1) * CH], zero_sb, at_sb[:, 0, c * CH:(c + 1) * CH],
                              start=False, stop=True).then_inc(s_y, 1)
                pe.wait_ge(s_yc, C)
                for t in range(T):
                    tr = pe.transpose(psA[:, t * P:(t + 1) * P], t_sb[:, t * P:(t + 1) * P], ident)
                    if t % 4 == 3:
                        tr.then_inc(s_yn, 1)
                for c in range(C):
                    for t in range(4 * c, 4 * c + 4):
                        pe.matmul(psB[:, t * P:(t + 1) * P], x_sb[:, t, :], ident, start=(t % 4 == 0), stop=False)
                pe.wait_ge(s_ync, C)
                propagate(psB, True)


def build(nc, x, adjT, W0, b0, W1, a1, upper, plan, outT):
    b = buffers(nc, *x.shape)
    build_fast(nc, b, x, adjT, W0, b0, W1, a1, upper, plan, outT)
    build_general(nc, b, x, adjT, outT)


def kernel(x, adj, L0_gnn_W, L0_gnn_b, L1_gnn_W, L1_gnn_a):
    import concourse.bacc as bacc
    from concourse.bass_utils import run_bass_kernel_spmd

    x, adj, W0, b0, W1, a1 = (np.asarray(v) for v in (x, adj, L0_gnn_W, L0_gnn_b, L1_gnn_W, L1_gnn_a))
    F = x.shape[1]
    arrays = {
        "x": x, "adjT": np.ascontiguousarray(adj.T), "W0": W0, "b0": b0.reshape(1, F), "W1": W1,
        "a1": np.ascontiguousarray(a1.reshape(2, F).T),
    }
    T = x.shape[0] // P
    p = np.arange(P)[:, None]
    arrays["upper"] = (p < p.T).astype(np.float32)
    arrays["plan"] = np.concatenate([
        p.T + 0 * p, P * np.arange(T)[None, :] + 0 * p,
        (p % 2 == 0), (p % 2 == 1), (p == 2) + np.zeros((1, P)),
    ], axis=1).astype(np.float32)
    nc = bacc.Bacc("TRN2", target_bir_lowering=False, num_devices=1)
    args = [nc.dram_tensor(n, v.shape, mybir.dt.from_np(v.dtype), kind="ExternalInput").ap()
            for n, v in arrays.items()]
    out = nc.dram_tensor("outT", (F, x.shape[0]), FP32, kind="ExternalOutput").ap()
    build(nc, *args, out)
    r = run_bass_kernel_spmd(nc, [arrays], core_ids=[0])
    return np.ascontiguousarray(r.results[0]["outT"].T)
```
